# Optimizing a Trainium2 kernel written in Bass

```python
import numpy as np
import jax
import jax.numpy as jnp

def _softmax(x, axis=-1):
    return jax.nn.softmax(x, axis=axis)
def _gelu(x):
    return jax.nn.gelu(x, approximate=True)
def _silu(x):
    return jax.nn.silu(x)
def _sigmoid(x):
    return jax.nn.sigmoid(x)
def _layernorm(x, axis=-1, eps=1e-5):
    m = jnp.mean(x, axis=axis, keepdims=True)
    v = jnp.var(x, axis=axis, keepdims=True)
    return (x - m) / jnp.sqrt(v + eps)
def _scatter_add(tgt, idx, src, axis=0):
    return tgt.at[idx].add(src)
def _segment_sum(src, seg, n):
    return jax.ops.segment_sum(src, seg, n)

kernel_name = 'mk_adj_preln_d1_adj_128_a03a24'

def setup_inputs(seed: int = 0):
    np.random.seed(seed)
    _w = jnp.asarray
    def _rec_inputs():
        import jax
        import jax.numpy as jnp
        _gk = jax.random.key(seed)
        x = -0.000929 + 1 * jax.random.normal(jax.random.fold_in(_gk, 1), (8192, 128), jnp.float32)
        _a = jax.random.bernoulli(jax.random.fold_in(_gk, 2), 0.000976562, (8192, 8192))
        _a = jnp.logical_or(_a, jnp.eye(8192, dtype=bool))
        _af = _a.astype(jnp.float32)
        _af = _af * jax.random.uniform(jax.random.fold_in(_gk, 3), (8192, 8192), jnp.float32, 0.05, 1e+09)
        adj = _af
        return x, adj
    x, adj = _rec_inputs()
    def _L0_gnn_setup():
        import jax, jax.numpy as jnp
        import numpy as np
        N, F_IN, F_OUT, H = (8192, 128, 128, 4)
        NEG = -1000000000.0
        key = jax.random.key(seed)
        k1, k2, k3, k4, k5 = jax.random.split(key, 5)
        x = jax.random.normal(k1, (N, F_IN), dtype=jnp.float32)
        edge = jax.random.uniform(k2, (N, N)) < 0.05
        mask = jnp.where(edge, 0.0, NEG).astype(jnp.float32)

        def xavier(k, shape, fan_in, fan_out):
            lim = float(np.sqrt(6.0 / (fan_in + fan_out)))
            return jax.random.uniform(k, shape, minval=-lim, maxval=lim, dtype=jnp.float32)
        W = xavier(k3, (H, F_IN, F_OUT), F_IN, F_OUT)
        a_src = xavier(k4, (H, F_OUT), F_OUT, 1)
        a_tgt = xavier(k5, (H, F_OUT), F_OUT, 1)
        return {'x': x, 'mask': mask, 'W': W, 'a_src': a_src, 'a_tgt': a_tgt}
    _L0_gnn_all = _L0_gnn_setup()
    _L0_gnn_in = {k: v for k, v in _L0_gnn_all.items() if k in ('W', 'a_src', 'a_tgt', )}
    del _L0_gnn_all

    return {
        "x": x,
        "adj": adj,
        "L0_gnn_W": _L0_gnn_in["W"],
        "L0_gnn_a_src": _L0_gnn_in["a_src"],
        "L0_gnn_a_tgt": _L0_gnn_in["a_tgt"],
    }

def reference(x, adj, L0_gnn_W, L0_gnn_a_src, L0_gnn_a_tgt):
    import jax
    import jax.numpy as jnp
    def _L0_gnn_ref(x, mask, W, a_src, a_tgt):
        import jax, jax.numpy as jnp
        import numpy as np
        N, F_IN, F_OUT, H = (8192, 128, 128, 4)
        NEG = -1000000000.0
        proj = jnp.einsum('nf,hfo->hno', x, W)
        s_src = jnp.einsum('hno,ho->hn', proj, a_src)
        s_tgt = jnp.einsum('hno,ho->hn', proj, a_tgt)
        scores = jax.nn.leaky_relu(s_src[:, :, None] + s_tgt[:, None, :], negative_slope=0.2)
        attn = jax.nn.softmax(mask[None, :, :] + scores, axis=1)
        vals = jnp.einsum('hij,hjo->hio', attn, proj)
        vals = vals + x[None, :, :]
        vals = jax.nn.elu(vals)
        return vals.mean(axis=0)

    h = jnp.maximum(_layernorm(x, axis=-1), 0.0)
    x = x + _L0_gnn_ref(h, adj, L0_gnn_W, L0_gnn_a_src, L0_gnn_a_tgt)
    return x


_drawn_inputs = setup_inputs


def setup_inputs(seed=0):
    import zlib

    import numpy as np

    out = dict(_drawn_inputs(seed))
    spreads = {}
    factors = {}
    for name, (base, spread) in spreads.items():
        noise = np.random.default_rng([zlib.crc32(name.encode()), seed]).standard_normal(out[name].shape)
        drawn = base * np.exp(spread * noise) if base else spread * noise
        out[name] = jnp.asarray(drawn.astype(out[name].dtype))
    for name, factor in factors.items():
        out[name] = (out[name] * factor).astype(out[name].dtype)
    return out
```

```python
from contextlib import ExitStack

import concourse.bass as bass
from concourse import mybir

P = 128
F32 = mybir.dt.float32
I32 = mybir.dt.int32
ALU = mybir.AluOpType
ACT = mybir.ActivationFunctionType
AX = mybir.AxisListType
EPS = 1e-5
SLOPE = 0.2


def gat_kernel(nc, x, adj, W, a_src, a_tgt, out):
    N, F = x.shape
    H, _, O = W.shape
    NT = N // P
    CH = 8
    NC = NT // CH
    assert F == P and O == P and H * O == 512 and NT % (2 * CH) == 0

    with ExitStack() as ctx:
        def sb(name, shape, dt=F32):
            return ctx.enter_context(nc.sbuf_tensor(name, shape, dt))

        def ps(name, shape, dt=F32):
            return ctx.enter_context(nc.psum_tensor(name, shape, dt))

        def sem(name):
            return ctx.enter_context(nc.semaphore(name))

        h = sb("h", [P, NT, F])
        w_sb = sb("w_sb", [P, H, O])
        wst = sb("wst", [P, 2 * H])
        ident = sb("ident", [P, P])
        ones = sb("ones", [P, P])
        mean = sb("mean", [P, NT])
        var = sb("var", [P, NT])
        half = sb("half", [P, NT])
        big = sb("big", [P, H * NT * P])
        flag = sb("flag", [1, 1], I32)
        a_bc = big[:, 0:2 * H * O].rearrange("p (k h o) -> p k h o", k=2, h=H)
        a_w = big[:, 2 * H * O:4 * H * O].rearrange("p (k h o) -> p k h o", k=2, h=H)
        stats = big[:, 4 * H * O:4 * H * O + NT * 6].rearrange("p (t c) -> p t c", c=6)

        x_t = x.rearrange("(t p) f -> p t f", p=P)
        out_t = out.rearrange("(t p) f -> p t f", p=P)
        adj_t = adj.rearrange("(t p) j -> p t j", p=P)

        s_x = sem("s_x_loaded")
        s_w = sem("s_weights_loaded")
        s_ones = sem("s_ones")
        s_ident = sem("s_ident")
        s_dve = sem("s_setup_vector")
        s_sqrt = sem("s_sqrt")

        with nc.Block() as block:
            @block.sync
            def _(sp):
                sp.dma_start(h[:, :, :], x_t).then_inc(s_x, 16)
                sp.dma_start(w_sb[:, :, :], W.rearrange("h f o -> f h o")).then_inc(s_w, 16)
                sp.dma_start(a_bc[:, 0, :, :], a_src.partition_broadcast(P)).then_inc(s_w, 16)
                sp.dma_start(a_bc[:, 1, :, :], a_tgt.partition_broadcast(P)).then_inc(s_w, 16)

            @block.gpsimd
            def _(pool):
                pool.memset(flag[:, :], 1)
                pool.memset(ones[:, :], 1.0).then_inc(s_ones, 1)
                pool.wait_ge(s_ones, 1)
                pool.affine_select(ident[:, :], ones[:, :], pattern=[[-1, P]], compare_op=ALU.is_equal,
                                   fill=0.0, base=0, channel_multiplier=1).then_inc(s_ident, 1)

            @block.scalar
            def _(act):
                act.wait_ge(s_dve, 5)
                act.activation(half[:, :], var[:, :], ACT.Sqrt).then_inc(s_sqrt, 1)

            @block.vector
            def _(dve):
                dve.wait_ge(s_w, 48)
                for k in range(2):
                    ins = dve.tensor_tensor(a_w[:, k], w_sb[:, :, :], a_bc[:, k], ALU.mult)
                ins.then_inc(s_dve, 1)
                dve.wait_ge(s_dve, 1)
                dve.tensor_reduce(wst[:, :], a_w.rearrange("p k h o -> p (k h) o"), AX.X, ALU.add)
                dve.wait_ge(s_x, 16)
                for t in range(NT):
                    ins = dve.bn_stats(stats[:, t, :], h[:, t, :])
                ins.then_inc(s_dve, 1)
                dve.wait_ge(s_dve, 2)
                me, qe, mo, qo = (stats[:, :, c] for c in (1, 2, 4, 5))
                dve.tensor_tensor(mean[:, :], me, mo, ALU.add)
                dve.tensor_tensor(half[:, :], me, mo, ALU.subtract)
                dve.tensor_tensor(var[:, :], qe, qo, ALU.add).then_inc(s_dve, 1)
                dve.wait_ge(s_dve, 3)
                dve.tensor_scalar(mean[:, :], mean[:, :], 0.5, None, ALU.mult)
                dve.tensor_scalar(var[:, :], var[:, :], 1.0 / F, EPS, ALU.mult, ALU.add)
                dve.scalar_tensor_tensor(half[:, :], half[:, :], 0.25, half[:, :], ALU.mult, ALU.mult).then_inc(s_dve, 1)
                dve.wait_ge(s_dve, 4)
                dve.tensor_tensor(var[:, :], var[:, :], half[:, :], ALU.add).then_inc(s_dve, 1)
                dve.wait_ge(s_sqrt, 1)
                dve.reciprocal(var[:, :], half[:, :]).then_inc(s_dve, 1)
                dve.wait_ge(s_dve, 6)
                for t in range(NT):
                    ins = dve.tensor_scalar(h[:, t, :], h[:, t, :], mean[:, t:t + 1], var[:, t:t + 1],
                                            ALU.subtract, ALU.mult)
                ins.then_inc(s_dve, 1)
                dve.wait_ge(s_dve, 7)
                dve.tensor_scalar(h[:, :, :], h[:, :, :], 0.0, None, ALU.max)

        dense_path(nc, ctx, dict(N=N, H=H, O=O, NT=NT, CH=CH, NC=NC), h, w_sb, wst, ident, big, flag,
                   x_t, out_t, adj_t)


def dense_path(nc, ctx, dims, h, w_sb, wst, ident, big, flag, x_t, out_t, adj_t):
    N, H, O, NT, CH, NC = (dims[k] for k in ("N", "H", "O", "NT", "CH", "NC"))

    def sb(name, shape, dt=F32):
        return ctx.enter_context(nc.sbuf_tensor(name, shape, dt))

    def ps(name, shape, dt=F32):
        return ctx.enter_context(nc.psum_tensor(name, shape, dt))

    def sem(name):
        return ctx.enter_context(nc.semaphore(name))

    src_all = big[:, :].rearrange("p (h t i) -> p h t i", h=H, t=NT)
    proj = big[:, :].rearrange("p (t h o) -> p t h o", t=NT, h=H)
    nat = [sb(f"nat{b}", [P, CH * P]) for b in range(2)]
    z = sb("z", [P, H, CH, P])
    hc = sb("hc", [P, P])
    hT = sb("hT", [P, P])
    w_bc = sb("w_bc", [P, H, P])
    src_row = sb("src_row", [P, H, P])
    st = sb("st", [P, NT, 2 * H])
    smax = sb("smax", [P, H])
    nsmax = sb("nsmax", [P, NC, H])
    csum = sb("csum", [P, NC, H])
    nmax = sb("nmax", [P, NT, H])
    rsum = sb("rsum", [P, NT, H])
    xrow = sb("xrow", [P, O])
    fin = sb("fin", [P, O])
    v = sb("v", [P, H, O])
    e = sb("e", [P, H, O])

    pT = [ps(f"pT{b}", [P, CH, P]) for b in range(2)]
    pW = ps("pW", [P, H, P])
    pH = ps("pH", [P, P])
    pO = ps("pO", [P, H, O])

    d_wbc = sem("d_wbc")
    d_hc = sem("d_hc_copied")
    d_hps = sem("d_h_turned")
    d_hT = sem("d_hT_copied")
    d_small = sem("d_small_products")
    d_small_out = sem("d_small_products_read")
    d_nat = [sem(f"d_nat{b}_landed") for b in range(2)]
    d_turn = sem("d_adj_turned")
    d_zfree = sem("d_z_free")
    d_u = sem("d_u")
    d_l = sem("d_lrelu")
    d_z = sem("d_z_masked")
    d_s = sem("d_z_shifted")
    d_u2 = sem("d_step_max")
    d_e = sem("d_exp")
    d_comb = sem("d_combine")
    d_combe = sem("d_combine_exp")
    d_v = sem("d_final_sum")
    d_ve = sem("d_final_exp")
    d_f = sem("d_final_steps")
    d_fin = sem("d_final_ready")
    d_x = sem("d_xrow_landed")
    d_out = sem("d_out_stored")

    S1 = NT * NC
    COMB = 4
    FINAL = 4

    def dense(eng, program):
        go = eng.value_load(flag[0:1, 0:1], min_val=0, max_val=1)
        with eng.If(go > 0):
            program(eng)

    def dense_sync(sp):
        sp.sem_inc(d_out, 16)
        with sp.Fori(0, NT) as j:
            with sp.Fori(0, NC // 2) as c:
                for b in range(2):
                    n = j * NC + c * 2 + b
                    sp.wait_ge(d_turn, n + 1)
                    sp.dma_start(nat[b][:, :].rearrange("p (c j) -> p c j", c=CH),
                                 adj_t[:, bass.ds((c * 2 + b) * CH, CH), bass.ds(j * P, P)]).then_inc(d_nat[b], 16)
        with sp.Fori(0, NT) as t:
            sp.wait_ge(d_fin, t + 1)
            sp.dma_start(xrow[:, :], x_t[:, t, :]).then_inc(d_x, 16)
            with sp.Fori(0, NC // 2) as g:
                for b in range(2):
                    n = t * NC + g * 2 + b + S1
                    sp.wait_ge(d_turn, n + 1)
                    sp.dma_start(nat[b][:, :], adj_t[:, t, bass.ds((g * 2 + b) * CH * P, CH * P)]).then_inc(d_nat[b], 16)
            sp.wait_ge(d_fin, t + 2)
            sp.dma_start(out_t[:, t, :], fin[:, :]).then_inc(d_out, 16)
        sp.wait_ge(d_out, (NT + 1) * 16)

    def dense_tensor(pe):
        def turn_h(k):
            pe.wait_ge(d_hc, k + 1)
            pe.transpose(pH[:, :], hc[:, :], ident[:, :]).then_inc(d_hps, 1)
            pe.wait_ge(d_hT, k + 1)

        def spread_src():
            for hd in range(H):
                mm = pe.matmul(pW[:, hd, :], w_bc[:, hd, :], hT[:, :], start=True, stop=True, skip_group_check=True)
            return mm

        def turn_adj(n, b, cycle):
            pe.wait_ge(d_nat[b], (cycle + 1) * 16)
            pe.wait_ge(d_z, n + 1)
            for c in range(CH):
                mm = pe.transpose(pT[b][:, c, :], nat[b][:, c * P:(c + 1) * P], ident[:, :])
            mm.then_inc(d_turn, 1)

        pe.sem_inc(d_turn, 2)
        pe.wait_ge(d_wbc, 1)
        with pe.Fori(0, NT) as t:
            turn_h(t)
            spread_src()
            pe.matmul(pH[:, 0:2 * H], hT[:, :], wst[:, :], start=True, stop=True).then_inc(d_small, 1)
        with pe.Fori(0, NT) as j:
            with pe.Fori(0, NC // 2) as c:
                for b in range(2):
                    turn_adj(j * NC + c * 2 + b, b, j * (NC // 2) + c)
        with pe.Fori(0, NT) as t:
            turn_h(t + NT)
            pe.matmul(pW[:, :, :], hT[:, :], w_sb[:, :, :].rearrange("f h o -> f (h o)"),
                      start=True, stop=True).then_inc(d_small, 1)
        with pe.Fori(0, NT) as t:
            turn_h(t + 2 * NT)
            spread_src().then_inc(d_small, 1)
            pe.wait_ge(d_v, t + 1)
            for gg in range(NC // 2):
                for b in range(2):
                    g = gg * 2 + b
                    n = t * NC + g + S1
                    turn_adj(n, b, (t + NT) * (NC // 2) + gg)
                    pe.wait_ge(d_e, t * NC + g + 1)
                    for c in range(CH):
                        for hd in range(H):
                            mm = pe.matmul(pO[:, hd, :], z[:, hd, c, :], proj[:, g * CH + c, hd, :],
                                           start=(g == 0 and c == 0 and hd == 0), stop=(g == NC - 1 and c == CH - 1),
                                           skip_group_check=True)
                    mm.then_inc(d_zfree, 1)

    def dense_scalar(act):
        def copy_h(k, t):
            act.copy(hc[:, :], h[:, t, :]).then_inc(d_hc, 1)
            act.wait_ge(d_hps, k + 1)
            act.copy(hT[:, :], pH[:, :]).then_inc(d_hT, 1)
            act.wait_ge(d_small, k + 1)
        with act.Fori(0, NT) as t:
            copy_h(t, t)
            act.copy(src_all[:, :, t, :], pW[:, :, :])
            act.copy(st[:, t, :], pH[:, 0:2 * H]).then_inc(d_small_out, 1)
        with act.Fori(0, NT) as j:
            with act.Fori(0, NC) as c:
                n = j * NC + c
                act.wait_ge(d_s, n + 1)
                for hd in range(H):
                    ins = act.activation(z[:, hd], z[:, hd], ACT.Exp, bias=nsmax[:, c, hd:hd + 1],
                                         accum_out=csum[:, c, hd:hd + 1])
                ins.then_inc(d_zfree, 1)
            act.wait_ge(d_comb, j * COMB + 2)
            act.activation(nsmax[:, :, :], nsmax[:, :, :], ACT.Exp).then_inc(d_combe, 1)
        with act.Fori(0, NT) as t:
            copy_h(t + NT, t)
            act.wait_ge(d_comb, NT * COMB + t + 2)
        with act.Fori(0, NT) as t:
            copy_h(t + 2 * NT, t)
            act.copy(src_row[:, :, :], pW[:, :, :]).then_inc(d_small_out, 1)
            with act.Fori(0, NC) as g:
                n = t * NC + g + S1
                act.wait_ge(d_s, n + 1)
                act.activation(z[:, :, :, :], z[:, :, :, :], ACT.Exp).then_inc(d_e, 1)
            act.wait_ge(d_v, t + 2)
            act.activation(e[:, :, :], v[:, :, :], ACT.Exp).then_inc(d_ve, 1)

    def dense_vector(dve):
        def scores(n, src, tgt, T):
            dve.wait_ge(d_zfree, n + 1)
            dve.tensor_tensor(z[:, :, :, :], src, tgt, ALU.add).then_inc(d_u, 1)
            dve.wait_ge(d_u, n + 1)
            dve.scalar_tensor_tensor(z[:, :, :, :], z[:, :, :, :], SLOPE, z[:, :, :, :],
                                     ALU.mult, ALU.max).then_inc(d_l, 1)
            dve.wait_ge(d_l, n + 1)
            dve.wait_ge(d_turn, n + 3)
            dve.tensor_tensor(z[:, :, :, :], z[:, :, :, :],
                              T[:, :, :].rearrange("p (g c) i -> p g c i", g=1).to_broadcast([P, H, CH, P]),
                              ALU.add).then_inc(d_z, 1)
            dve.wait_ge(d_z, n + 3)

        dve.sem_inc(d_z, 2)
        dve.sem_inc(d_zfree, 1)
        dve.sem_inc(d_v, 1)
        dve.sem_inc(d_fin, 1)
        for hd in range(H):
            ins = dve.tensor_copy(w_bc[:, hd, :], wst[:, hd:hd + 1].to_broadcast([P, P]))
        ins.then_inc(d_wbc, 1)
        dve.wait_ge(d_small_out, NT)
        with dve.Fori(0, NT) as j:
            with dve.Fori(0, NC // 2) as cc:
                for b in range(2):
                    c = cc * 2 + b
                    n = j * NC + c
                    scores(n, src_all[:, :, bass.ds(c * CH, CH), :],
                           st[:, j, H:2 * H].unsqueeze(2).unsqueeze(3).to_broadcast([P, H, CH, P]), pT[b])
                    dve.tensor_reduce(smax[:, :], z[:, :, :, :].rearrange("p h c i -> p h (c i)"), AX.X,
                                      ALU.max).then_inc(d_u2, 1)
                    dve.wait_ge(d_u2, n + 1)
                    dve.tensor_scalar(nsmax[:, c, :], smax[:, :], -1.0, None, ALU.mult).then_inc(d_s, 1)
            dve.wait_ge(d_zfree, j * NC + NC + 1)
            dve.tensor_reduce(nmax[:, j, :], nsmax[:, :, :].rearrange("p c h -> p h c"), AX.X,
                              ALU.min).then_inc(d_comb, 1)
            dve.wait_ge(d_comb, j * COMB + 1)
            dve.scalar_tensor_tensor(nsmax[:, :, :], nsmax[:, :, :], -1.0,
                                     nmax[:, j, :].unsqueeze(1).to_broadcast([P, NC, H]),
                                     ALU.mult, ALU.add).then_inc(d_comb, 1)
            dve.wait_ge(d_combe, j + 1)
            dve.tensor_tensor(csum[:, :, :], csum[:, :, :], nsmax[:, :, :], ALU.mult).then_inc(d_comb, 1)
            dve.wait_ge(d_comb, j * COMB + 3)
            dve.tensor_reduce(rsum[:, j, :], csum[:, :, :].rearrange("p c h -> p h c"), AX.X,
                              ALU.add).then_inc(d_comb, 1)
        dve.wait_ge(d_comb, NT * COMB)
        dve.reciprocal(rsum[:, :, :], rsum[:, :, :]).then_inc(d_comb, 1)
        dve.wait_ge(d_comb, NT * COMB + 1)
        with dve.Fori(0, NT) as t:
            dve.wait_ge(d_small, t + NT + 1)
            dve.tensor_tensor(proj[:, t], pW[:, :, :], rsum[:, t, :].unsqueeze(2).to_broadcast([P, H, O]),
                              ALU.mult).then_inc(d_comb, 1)
        with dve.Fori(0, NT) as t:
            dve.wait_ge(d_small_out, t + NT + 1)
            for gg in range(NC // 2):
                for b in range(2):
                    n = t * NC + gg * 2 + b + S1
                    tiles = slice((gg * 2 + b) * CH, (gg * 2 + b + 1) * CH)
                    scores(n, src_row[:, :, :].unsqueeze(2).to_broadcast([P, H, CH, P]),
                           st[:, tiles, H:2 * H].rearrange("p c h -> p h c").unsqueeze(3).to_broadcast([P, H, CH, P]),
                           pT[b])
                    dve.tensor_tensor(z[:, :, :, :], z[:, :, :, :],
                                      nmax[:, tiles, :].rearrange("p c h -> p h c").unsqueeze(3).to_broadcast([P, H, CH, P]),
                                      ALU.add).then_inc(d_s, 1)
            dve.wait_ge(d_zfree, (t + 1) * NC + S1 + 1)
            dve.tensor_tensor(v[:, :, :], pO[:, :, :], h[:, t, :].unsqueeze(1).to_broadcast([P, H, O]),
                              ALU.add).then_inc(d_v, 1)
            dve.wait_ge(d_ve, t + 1)
            dve.tensor_scalar(e[:, :, :], e[:, :, :], 1.0, -1.0, ALU.min, ALU.add).then_inc(d_f, 1)
            dve.wait_ge(d_f, t * FINAL + 1)
            dve.tensor_tensor(v[:, :, :], v[:, :, :], e[:, :, :], ALU.max).then_inc(d_f, 1)
            dve.wait_ge(d_f, t * FINAL + 2)
            dve.tensor_tensor(v[:, 0:2, :], v[:, 0:2, :], v[:, 2:4, :], ALU.add).then_inc(d_f, 1)
            dve.wait_ge(d_f, t * FINAL + 3)
            dve.tensor_tensor(v[:, 0, :], v[:, 0, :], v[:, 1, :], ALU.add).then_inc(d_f, 1)
            dve.wait_ge(d_f, t * FINAL + 4)
            dve.wait_ge(d_x, (t + 1) * 16)
            dve.wait_ge(d_out, (t + 1) * 16)
            dve.scalar_tensor_tensor(fin[:, :], v[:, 0, :], 1.0 / H, xrow[:, :], ALU.mult, ALU.add).then_inc(d_fin, 1)

    with nc.Block() as block:
        @block.sync
        def _(sp):
            dense(sp, dense_sync)

        @block.tensor
        def _(pe):
            dense(pe, dense_tensor)

        @block.scalar
        def _(act):
            dense(act, dense_scalar)

        @block.vector
        def _(dve):
            dense(dve, dense_vector)


_INS = ["x", "adj", "L0_gnn_W", "L0_gnn_a_src", "L0_gnn_a_tgt"]


def kernel(**inputs):
    import numpy as np
    import concourse.bacc as bacc
    from concourse.bass_utils import run_bass_kernel_spmd

    nc = bacc.Bacc("TRN2", target_bir_lowering=False, num_devices=1)
    arrays, args = {}, []
    for name in _INS:
        a = np.ascontiguousarray(inputs[name])
        arrays[f"in_{name}"] = a
        args.append(nc.dram_tensor(f"in_{name}", a.shape, mybir.dt.from_np(a.dtype), kind="ExternalInput").ap())
    shape = inputs["x"].shape
    args.append(nc.dram_tensor("out", shape, F32, kind="ExternalOutput").ap())
    gat_kernel(nc, *args)
    r = run_bass_kernel_spmd(nc, [arrays], core_ids=[0])
    return r.results[0]["out"]
```

```python
from contextlib import ExitStack

import concourse.bass as bass
from concourse import mybir

P = 128
F32 = mybir.dt.float32
F16 = mybir.dt.float16
FP8 = mybir.dt.float8e5
I32 = mybir.dt.int32
ALU = mybir.AluOpType
ACT = mybir.ActivationFunctionType
AX = mybir.AxisListType
EPS = 1e-5
SLOPE = 0.2

KAPPA = 2.0 ** -5
GAP = 16.5 / KAPPA
UNDERFLOW = 105.0
ROUNDING = 2.0 ** -22
HSCALE = 2.0 ** 12


class Arena:

    def __init__(self, tensor, start=0):
        self.tensor, self.at = tensor, start

    def take(self, dims, dt=F32, size=4):
        count = 1
        for d in dims:
            count *= d
        words = count * size // 4
        assert self.at + words <= self.tensor.shape[1], (self.at, words)
        v = self.tensor[:, self.at:self.at + words]
        self.at += words
        if size != 4:
            v = v.bitcast(dt)
        names = "abcd"[:len(dims)]
        if len(dims) > 1:
            v = v.rearrange("p (" + " ".join(names) + ") -> p " + " ".join(names),
                            **{n: d for n, d in zip(names, dims)})
        return v


def gat_kernel(nc, x, adj, W, a_src, a_tgt, out):
    N, F = x.shape
    H, _, O = W.shape
    NT = N // P
    CH = 8
    NC = NT // CH
    assert F == P and O == P and H * O == 512 and NT % (2 * CH) == 0

    with ExitStack() as ctx:
        def sb(name, shape, dt=F32):
            return ctx.enter_context(nc.sbuf_tensor(name, shape, dt))

        c = dict(N=N, F=F, H=H, O=O, NT=NT, CH=CH, NC=NC)
        c["w_sb"] = sb("w_sb", [P, H, O])
        c["wst"] = sb("wst", [P, 2 * H])
        c["ident"] = sb("ident", [P, P])
        c["ones"] = sb("ones", [P, P])
        c["mean"] = sb("mean", [P, NT])
        c["rstd"] = sb("rstd", [P, NT])
        c["nmr"] = sb("nmr", [P, NT])
        c["flag"] = sb("flag", [1, 1], I32)
        c["arena"] = sb("arena", [P, 52150])
        c["x_t"] = x.rearrange("(t p) f -> p t f", p=P)
        c["out_t"] = out.rearrange("(t p) f -> p t f", p=P)
        c["adj_t"] = adj.rearrange("(t p) j -> p t j", p=P)
        c["psum"] = [ctx.enter_context(nc.psum_tensor(f"ps{b}", [P, 1024], F32)) for b in range(4)]

        peaked_path(nc, ctx, c, W, a_src, a_tgt)
        dense_path(nc, ctx, c)


def peaked_path(nc, ctx, c, W, a_src, a_tgt):
    F, H, O, NT = (c[k] for k in ("F", "H", "O", "NT"))
    w_sb, wst, ident, ones, mean, rstd, nmr, flag = (
        c[k] for k in ("w_sb", "wst", "ident", "ones", "mean", "rstd", "nmr", "flag"))
    x_t, out_t, adj_t = (c[k] for k in ("x_t", "out_t", "adj_t"))
    NP = 4
    PT = NT // NP
    G = 8
    NG = NT // G
    RT = NT // G
    RC = RT * P
    LAST_MAX = 5

    def sem(name):
        return ctx.enter_context(nc.semaphore(name))

    A = Arena(c["arena"])
    acc = A.take([NT, P])
    h4 = A.take([NT, F])
    units = A.take([G, G, RC], FP8, 1)
    strips = A.take([2, NT, P])
    S0 = A.at - 2 * NT * P
    rowmax = A.take([2, P])
    PARTS = A.at
    parts = A.take([2, G, 2, F], F16, 2)
    cert = A.take([2, G + 1])
    hist = A.take([NT, G + 1])
    cmx = A.take([2])
    small = A.take([4])
    bad = A.take([4])
    tot = A.take([NT])
    wsq = A.take([2 * H])
    flag_f = A.take([1])
    B = Arena(c["arena"])
    a_bc = B.take([2, H, O])
    a_w = B.take([2, H, O])
    L = Arena(c["arena"], PARTS)
    stats = L.take([NT, 6])
    half = L.take([NT])
    var = L.take([NT])
    D = Arena(c["arena"], S0)
    BT = 4
    x_rows = D.take([2, RT, F])
    stage = D.take([2, RC])
    v = D.take([2, BT, H, O])
    e = D.take([2, H, O])
    s2 = D.take([2, BT, 2, O])
    s1 = D.take([2, BT, O])
    osb = D.take([2, RT, O])


    turned_ps = [c["psum"][b][:, :].rearrange("p (t i) -> p t i", i=P) for b in range(2)]
    prod_ps = [c["psum"][2 + b] for b in range(2)]
    proj_ps = [c["psum"][b // 2][:, (b % 2) * 512:(b % 2 + 1) * 512] for b in range(4)]

    s_w = sem("weights_landed")
    s_x = [sem(f"x{i}_landed") for i in range(NP)]
    s_ones = sem("ones_set")
    s_ident = sem("ident_set")
    s_set = sem("setup_vector")
    s_sqrt = sem("setup_sqrt")
    s_stat = sem("layernorm_statistics")
    s_pool = sem("layernorm_steps")
    s_acc0 = sem("acc_cleared")
    s_hi = sem("high_parts")
    s_parts = sem("parts_ready")
    f_kept = sem("cert_kept")
    f_in = [sem(f"strip_piece{i}_landed") for i in range(2 * NP)]
    f_turn = sem("range_turned")
    f_exp = sem("range_exped")
    f_max = sem("half_strip_max")
    f_mt = sem("maxima_turned")
    f_mx = sem("column_max")
    f_nb = sem("bias_ready")
    f_prod = sem("range_product")
    f_acc = sem("range_added")
    w_pe = sem("waited_tensor")
    w_act = sem("waited_scalar")
    w_pool = sem("waited_gpsimd")
    t_x = [sem(f"x_rows{b}_landed") for b in range(2)]
    t_p = sem("tail_projected")
    t_v = sem("tail_v")
    t_e = sem("tail_exp")
    t_u = sem("tail_exp_below_one")
    t_m = sem("tail_elu")
    t_s2 = sem("tail_two_heads")
    t_s1 = sem("tail_head_sum")
    t_o = sem("tail_rows")
    t_out = [sem(f"tail_stored{b}") for b in range(2)]
    g_d = sem("check_vector")
    g_n = sem("check_norms")
    g_b = sem("check_turned")

    def unit(parity, k, r):
        return units[:, k, r, :] if parity == 0 else units[:, r, k, :]

    def order(s, r):
        place = LAST_MAX + 1 if r == G else r + (r > LAST_MAX)
        return (1 + (G + 1) * s + place) % 2

    def strips_of(engine, body, before_products=None):
        def group(g, parity, product, strips_here):
            for k in strips_here:
                body(g, parity, k, k % 2, product, k == G - 1 and isinstance(g, int) and g == NG - 1)
        group(0, 0, False, range(G))
        if before_products:
            before_products()
        with engine.Fori(0, (NG - 2) // 2) as gg:
            group(gg * 2 + 1, 1, True, range(G))
            group(gg * 2 + 2, 0, True, range(G))
        group(NG - 1, 1, True, range(G))

    def tail_of(engine, body):
        with engine.Fori(0, G // 2 - 1) as kk:
            body(kk, True)
        body(G // 2 - 1, False)

    NB = 2 * RT // BT
    CHECKS = 18

    with nc.Block() as block:
        @block.sync
        def _(sp):
            sp.sem_inc(f_turn, 2 * G)
            def strip(s, q):
                for i in range(NP):
                    sp.wait_ge(f_turn, s * G + (i + 1) * (G // NP))
                    sp.dma_start(strips[:, q, i * PT:(i + 1) * PT, :],
                                 adj_t[:, i * PT:(i + 1) * PT, bass.ds(s * P, P)]).then_inc(f_in[q * NP + i], 16)
            strip(0, 0)
            sp.dma_start(w_sb[:, :, :], W.rearrange("h f o -> f h o")).then_inc(s_w, 16)
            sp.dma_start(a_bc[:, 0], a_src.partition_broadcast(P)).then_inc(s_w, 16)
            sp.dma_start(a_bc[:, 1], a_tgt.partition_broadcast(P)).then_inc(s_w, 16)
            for i in range(NP):
                sp.dma_start(h4[:, i * PT:(i + 1) * PT, :], x_t[:, i * PT:(i + 1) * PT, :]).then_inc(s_x[i], 16)
            strip(1, 1)
            with sp.Fori(1, NT // 2) as ss:
                for q in range(2):
                    strip(ss * 2 + q, q)
            sp.wait_ge(f_turn, (NT + 2) * G)
            for q in range(2):
                sp.dma_start(x_rows[:, q], x_t[:, q * RT:(q + 1) * RT, :]).then_inc(t_x[q], 16)
            def tail(kk, more):
                for q in range(2):
                    sp.wait_ge(t_o, (kk * 2 + q + 1) * (RT // BT))
                    if more:
                        sp.dma_start(x_rows[:, q], x_t[:, bass.ds((kk * 2 + q + 2) * RT, RT), :]).then_inc(t_x[q], 16)
                    sp.dma_start(out_t[:, bass.ds((kk * 2 + q) * RT, RT), :], osb[:, q]).then_inc(t_out[q], 16)
            tail_of(sp, tail)
            for q in range(2):
                sp.wait_ge(t_out[q], 16 * (G // 2 + 1))

        @block.gpsimd
        def _(pool):
            pool.sem_inc(t_s1, 2)
            pool.sem_inc(t_out[0], 16)
            pool.sem_inc(t_out[1], 16)
            pool.memset(ones[:, :], 1.0).then_inc(s_ones, 1)
            pool.wait_ge(s_ones, 1)
            pool.affine_select(ident[:, :], ones[:, :], pattern=[[-1, P]], compare_op=ALU.is_equal,
                               fill=0.0, base=0, channel_multiplier=1).then_inc(s_ident, 1)
            pool.sem_inc(f_kept, 2)
            pool.wait_ge(s_set, 2)
            pool.memset(acc, 0.0).then_inc(s_acc0, 1)
            halves = [slice(0, NT // 2), slice(NT // 2, NT)]

            def spread(a, half_):
                return a[:, half_].unsqueeze(2).to_broadcast([P, NT // 2, F])

            def layernorm_step(i):
                t = halves[i % 2]
                if i == 0:
                    pool.wait_ge(s_stat, 4)
                if i >= 2:
                    pool.wait_ge(s_pool, i - 1)
                if i < 2:
                    ins = pool.tensor_tensor(h4[:, t, :], h4[:, t, :], spread(rstd, t), ALU.mult)
                elif i < 4:
                    ins = pool.tensor_tensor(h4[:, t, :], h4[:, t, :], spread(nmr, t), ALU.add)
                else:
                    ins = pool.tensor_scalar(h4[:, t, :], h4[:, t, :], 0.0, HSCALE, ALU.max, ALU.mult)
                ins.then_inc(s_pool, 1)

            def split(g, parity):
                rows = h4[:, bass.ds(g * G, G), :]
                pool.tensor_copy(parts[:, parity, :, 0, :], rows).then_inc(s_hi, 1)
                pool.wait_ge(s_hi, g + 1)
                pool.sem_inc(w_pool, 1)
                pool.tensor_tensor(parts[:, parity, :, 1, :], rows, parts[:, parity, :, 0, :],
                                   ALU.subtract).then_inc(s_parts, 1)

            def strip(g, parity, k, q, product, is_last):
                pool.wait_ge(f_exp, (g * G + k + 1) * G + 2)
                pool.tensor_copy(hist[:, g * G + k, :], cert[:, q, :]).then_inc(f_kept, 1)
                if not product and k < 6:
                    layernorm_step(k)
                if k == 6:
                    if not product:
                        pool.wait_ge(s_pool, 6)
                    split(g, parity)
            strips_of(pool, strip)
            def tail(kk, more):
                for b in range(NB):
                    n = kk * (NB) + b
                    pool.wait_ge(t_m, (n + 1) * BT + 2)
                    pool.wait_ge(t_s1, n + 1)
                    pool.tensor_tensor(s2[:, b % 2], v[:, b % 2, :, 0:2, :], v[:, b % 2, :, 2:4, :], ALU.add).then_inc(t_s2, 1)
                    pool.wait_ge(t_s2, n + 3)
                    pool.tensor_tensor(s1[:, b % 2], s2[:, b % 2, :, 0, :], s2[:, b % 2, :, 1, :], ALU.add).then_inc(t_s1, 1)
            tail_of(pool, tail)

        @block.tensor
        def _(pe):
            def turn_maxima(s, b):
                pe.wait_ge(f_max, s * 2 + 2)
                for hf in range(2):
                    mm = pe.transpose(turned_ps[b][:, hf, :], rowmax[:, hf, :], ident[:, :])
                mm.then_inc(f_mt, 1)

            def product_part(block01, r, parity, out_ps):
                for part in range(2):
                    for n in range(RC // 512):
                        mm = pe.matmul(out_ps[:, n * 512:(n + 1) * 512], parts[:, parity, r, part, :],
                                       block01[:, n * 512:(n + 1) * 512],
                                       start=(r == 0 and part == 0), stop=(r == G - 1 and part == 1))
                return mm

            def strip(g, parity, k, q, product, is_last):
                s = g * G + k
                pe.wait_ge(f_exp, s * G + 1)
                if product and k == 0:
                    pe.wait_ge(s_parts, g)
                if product:
                    pe.wait_ge(f_acc, s - G + 1)
                    pe.sem_inc(w_pe, 1)
                done = 0
                for r in range(G):
                    while product and done < min(G, r + 2):
                        mm = product_part(unit(parity, k, done), done, 1 - parity, prod_ps[q])
                        done += 1
                        if done == G:
                            mm.then_inc(f_prod, 1)
                    if r == 1:
                        pe.wait_ge(f_mx, s + 1)
                        pe.wait_ge(f_exp, s * G + 2)
                    elif r == G - 1 and not is_last:
                        pe.wait_ge(f_mx, s + 2)
                    elif r > LAST_MAX:
                        pe.wait_ge(f_exp, s * G + r + 2 - (r == G - 1))
                    elif r > 1:
                        pe.wait_ge(f_exp, s * G + r + 1)
                    if r % (G // NP) == 0:
                        pe.wait_ge(f_in[q * NP + r // (G // NP)], (s - q) * 8 + 16)
                    for m in range(RT):
                        mm = pe.transpose(turned_ps[order(q, r)][:, m, :], strips[:, q, r * RT + m, :], ident[:, :])
                    mm.then_inc(f_turn, 1)
                    if r == LAST_MAX and not is_last:
                        pe.wait_ge(f_exp, s * G + LAST_MAX + 2)
                        turn_maxima(s + 1, order(q, G))

            def last_product(k, q):
                pe.wait_ge(f_acc, k + NT - G + 1)
                for r in range(G):
                    mm = product_part(unit(0, k, r), r, 1, prod_ps[q])
                mm.then_inc(f_prod, 1)

            def tail(k):
                pe.wait_ge(f_acc, k + NT - G + 3)
                for m in range(RT):
                    pe.wait_ge(t_v, k * RT + m + 1)
                    pe.matmul(proj_ps[m % 4], stage[:, k % 2, m * P:(m + 1) * P],
                              w_sb[:, :, :].rearrange("f h o -> f (h o)"), start=True, stop=True).then_inc(t_p, 1)
                    if k + 2 < G:
                        mm = product_part(unit(0, k + 2, m), m, 1, prod_ps[k % 2])
                        if m == G - 1:
                            mm.then_inc(f_prod, 1)

            pe.wait_ge(s_ident, 1)
            turn_maxima(0, 0)
            strips_of(pe, strip)
            pe.wait_ge(s_parts, NG)
            pe.wait_ge(f_exp, NT * G + 2)
            last_product(0, 0)
            pe.wait_ge(g_d, 1)
            pe.matmul(proj_ps[3][:, 0:2 * H], ones[:, :], wsq[:, :], start=True, stop=True).then_inc(g_n, 1)
            last_product(1, 1)
            pe.wait_ge(g_d, CHECKS - 2)
            pe.transpose(proj_ps[2][0:1, 0:P], bad[:, 0:1], ident[:, :]).then_inc(g_b, 1)
            pe.wait_ge(g_d, CHECKS)
            for k in range(G):
                tail(k)

        @block.scalar
        def _(act):
            def strip(g, parity, k, q, product, is_last):
                s = g * G + k
                act.wait_ge(f_nb, s + 1)
                act.wait_ge(f_kept, s + 1)
                for r in range(G):
                    act.wait_ge(f_turn, s * G + r + 1 + 2 * G)
                    act.sem_inc(w_act, 1)
                    act.activation(unit(parity, k, r), turned_ps[order(q, r)][:, :, :].rearrange("p t i -> p (t i)"),
                                   ACT.Exp, scale=KAPPA, bias=cert[:, q, G:G + 1],
                                   accum_out=cert[:, q, r:r + 1], saturate=False).then_inc(f_exp, 1)
                if not product and k == 0:
                    act.wait_ge(s_set, 4)
                    act.activation(half[:, :], var[:, :], ACT.Sqrt).then_inc(s_sqrt, 1)

            def tail(kk, more):
                for m in range(2 * RT):
                    n = kk * 2 * RT + m
                    act.wait_ge(t_v, n + 5)
                    act.wait_ge(t_m, n + 1)
                    act.activation(e[:, m % 2], v[:, m // BT % 2, m % BT], ACT.Exp).then_inc(t_e, 1)
                    act.wait_ge(t_e, n + 1)
                    act.activation(e[:, m % 2], e[:, m % 2], ACT.Relu, scale=-1.0, bias=1.0).then_inc(t_u, 1)

            act.sem_inc(f_exp, 2)
            strips_of(act, strip)
            tail_of(act, tail)

        @block.vector
        def _(dve):
            def strip_max(s, q, landed):
                for hf in range(2):
                    for i in range(NP // 2):
                        dve.wait_ge(f_in[q * NP + hf * NP // 2 + i], landed)
                    dve.tensor_reduce(rowmax[:, hf, :],
                                      strips[:, q, hf * NT // 2:(hf + 1) * NT // 2, :].rearrange("p t c -> p c t"),
                                      AX.X, ALU.max).then_inc(f_max, 1)

            def column_max(s, b, q):
                dve.wait_ge(f_mt, s + 1)
                dve.tensor_reduce(cmx[:, 0:1], turned_ps[b][:, 0:2, :], AX.XY, ALU.max).then_inc(f_mx, 1)
                dve.wait_ge(f_mx, s + 1)
                dve.wait_ge(f_kept, s + 1)
                dve.tensor_scalar(cert[:, q, G:G + 1], cmx[:, 0:1], -KAPPA, None, ALU.mult).then_inc(f_nb, 1)

            def strip(g, parity, k, q, product, is_last):
                s = g * G + k
                if not is_last:
                    strip_max(s + 1, 1 - q, (s + q) * 8 + 16)
                    column_max(s + 1, order(q, G), 1 - q)
                if not product and k == 0:
                    dve.wait_ge(s_sqrt, 1)
                    dve.reciprocal(rstd[:, :], half).then_inc(s_stat, 1)
                    dve.wait_ge(s_stat, 3)
                    dve.scalar_tensor_tensor(nmr[:, :], mean[:, :], -1.0, rstd[:, :], ALU.mult, ALU.mult).then_inc(s_stat, 1)
                if product:
                    dve.wait_ge(f_prod, s - G + 1)
                    rows = acc[:, k * RT:(k + 1) * RT, :].rearrange("p t i -> p (t i)")
                    dve.scalar_tensor_tensor(rows, prod_ps[q][:, :], 1.0 / HSCALE, rows,
                                             ALU.mult, ALU.add).then_inc(f_acc, 1)

            def last_add(k, q):
                dve.wait_ge(f_prod, k + NT - G + 1)
                dve.scalar_tensor_tensor(stage[:, q, :], prod_ps[q][:, :], 1.0 / HSCALE,
                                         acc[:, bass.ds(k * RT, RT), :].rearrange("p t i -> p (t i)"),
                                         ALU.mult, ALU.add).then_inc(f_acc, 1)

            def tail(kk, more, first=False):
                def elu(n, m):
                    dve.wait_ge(t_u, n + 1)
                    tile = v[:, m // BT % 2, m % BT]
                    dve.scalar_tensor_tensor(tile, e[:, m % 2], -1.0, tile, ALU.mult, ALU.max).then_inc(t_m, 1)
                def finish(m):
                    back = 1 if m < 0 else 0
                    b = m // BT + back * NB
                    q, at = b * BT // RT, b * BT % RT
                    dve.wait_ge(t_s1, (kk - back) * NB + b + 3)
                    dve.wait_ge(t_x[q], (kk - back + 1) * 16)
                    dve.wait_ge(t_out[q], (kk - back + 1) * 16)
                    dve.scalar_tensor_tensor(osb[:, q, at:at + BT, :], s1[:, b % 2], 1.0 / H,
                                             x_rows[:, q, at:at + BT, :], ALU.mult, ALU.add).then_inc(t_o, 1)
                for q in range(2):
                    for mq in range(RT):
                        m = q * RT + mq
                        n = kk * 2 * RT + m
                        if m % BT == 0 and not (first and m < 2 * BT):
                            finish(m - 2 * BT)
                        dve.wait_ge(t_p, n + 1)
                        if m % BT == 0:
                            dve.wait_ge(t_s2, kk * (NB) + m // BT + 1)
                        dve.scalar_tensor_tensor(v[:, m // BT % 2, m % BT],
                                                 h4[:, n, :].unsqueeze(1).to_broadcast([P, H, O]), 1.0 / HSCALE,
                                                 proj_ps[m % 4].rearrange("p (h o) -> p h o", h=H),
                                                 ALU.mult, ALU.add).then_inc(t_v, 1)
                        if m > 1:
                            elu(n - 2, m - 2)
                    if more:
                        last_add(kk * 2 + q + 2, q)
                for m in range(2 * RT - 2, 2 * RT):
                    elu(kk * 2 * RT + m, m)
                if not more:
                    finish(2 * RT - 2 * BT)
                    finish(2 * RT - BT)

            dve.sem_inc(f_acc, 2)
            dve.sem_inc(t_v, 4)
            dve.sem_inc(t_m, 2)
            dve.sem_inc(t_s2, 2)
            strip_max(0, 0, 16)
            column_max(0, 0, 0)
            dve.wait_ge(s_w, 48)
            for k in range(2):
                ins = dve.tensor_tensor(a_w[:, k], w_sb[:, :, :], a_bc[:, k], ALU.mult)
            ins.then_inc(s_set, 1)
            dve.wait_ge(s_set, 1)
            dve.tensor_reduce(wst[:, :].rearrange("p (k h) -> p k h", k=2), a_w, AX.X, ALU.add).then_inc(s_set, 1)
            dve.wait_ge(s_set, 2)
            dve.tensor_tensor(wsq, wst[:, :], wst[:, :], ALU.mult).then_inc(g_d, 1)
            for i in range(NP):
                dve.wait_ge(s_x[i], 16)
                for t in range(i * PT, (i + 1) * PT):
                    ins = dve.bn_stats(stats[:, t, :], h4[:, t, :])
            ins.then_inc(s_set, 1)
            dve.wait_ge(s_set, 3)
            me, qe, mo, qo = (stats[:, :, i] for i in (1, 2, 4, 5))
            dve.tensor_tensor(mean[:, :], me, mo, ALU.add)
            dve.tensor_tensor(half, me, mo, ALU.subtract)
            dve.tensor_tensor(var, qe, qo, ALU.add).then_inc(s_stat, 1)
            dve.wait_ge(s_stat, 1)
            dve.tensor_scalar(mean[:, :], mean[:, :], 0.5, None, ALU.mult)
            dve.tensor_scalar(var, var, 1.0 / F, EPS, ALU.mult, ALU.add)
            dve.scalar_tensor_tensor(half, half, 0.25, half, ALU.mult, ALU.mult).then_inc(s_stat, 1)
            dve.wait_ge(s_stat, 2)
            dve.tensor_tensor(var, var, half, ALU.add).then_inc(s_set, 1)

            strips_of(dve, strip, lambda: dve.wait_ge(s_acc0, 1))
            last_add(0, 0)

            dve.wait_ge(f_kept, NT + 2)
            lim, neg, nrm = small[:, 0:1], small[:, 1:2], small[:, 2:3]
            count = [1]

            def done(ins):
                ins.then_inc(g_d, 1)
                count[0] += 1
                dve.wait_ge(g_d, count[0])
            done(dve.tensor_reduce(tot, hist[:, :, 0:G], AX.X, ALU.add))
            done(dve.tensor_scalar(tot, tot, 1.0, None, ALU.not_equal))
            done(dve.tensor_reduce(bad[:, 1:2], tot, AX.X, ALU.max))
            done(dve.tensor_reduce(lim, hist[:, :, G], AX.X, ALU.max))
            done(dve.tensor_reduce(neg, hist[:, :, G], AX.X, ALU.min))
            done(dve.tensor_scalar(neg, neg, -1.0, None, ALU.mult))
            done(dve.tensor_tensor(lim, lim, neg, ALU.max))
            done(dve.tensor_scalar(lim, lim, -ROUNDING / KAPPA, GAP - UNDERFLOW, ALU.mult, ALU.add))
            done(dve.tensor_scalar(lim, lim, 0.0, None, ALU.max))
            done(dve.tensor_tensor(lim, lim, lim, ALU.mult))
            dve.wait_ge(g_n, 1)
            done(dve.tensor_reduce(nrm, proj_ps[3][:, 0:2 * H], AX.X, ALU.max))
            done(dve.tensor_scalar(nrm, nrm, 4.0 * F * 1.02, None, ALU.mult))
            done(dve.tensor_tensor(nrm, nrm, lim, ALU.is_lt))
            done(dve.tensor_scalar(bad[:, 2:3], nrm, -1.0, 1.0, ALU.mult, ALU.add))
            done(dve.tensor_tensor(bad[:, 0:1], bad[:, 1:2], bad[:, 2:3], ALU.max))
            dve.wait_ge(g_b, 1)
            done(dve.tensor_reduce(flag_f[0:1, 0:1], proj_ps[2][0:1, 0:P], AX.X, ALU.max))
            done(dve.tensor_copy(flag[:, :], flag_f[0:1, 0:1]))
            assert count[0] == CHECKS
            last_add(1, 1)
            tail(0, True, first=True)
            with dve.Fori(1, G // 2 - 1) as kk:
                tail(kk, True)
            tail(G // 2 - 1, False)


def dense_path(nc, ctx, c):
    N, H, O, NT, CH, NC = (c[k] for k in ("N", "H", "O", "NT", "CH", "NC"))
    w_sb, wst, ident, rstd, nmr, flag, x_t, out_t, adj_t = (
        c[k] for k in ("w_sb", "wst", "ident", "rstd", "nmr", "flag", "x_t", "out_t", "adj_t"))

    def sem(name):
        return ctx.enter_context(nc.semaphore(name))

    A = Arena(c["arena"])
    h = A.take([NT, P])
    big = A.take([H * NT * P])
    src_all = big.rearrange("p (h t i) -> p h t i", h=H, t=NT)
    proj = big.rearrange("p (t h o) -> p t h o", t=NT, h=H)
    nat = [A.take([CH * P]) for b in range(2)]
    z = A.take([H, CH, P])
    hc = A.take([P])
    hT = A.take([P])
    w_bc = A.take([H, P])
    src_row = A.take([H, P])
    st = A.take([NT, 2 * H])
    smax = A.take([H])
    nsmax = A.take([NC, H])
    csum = A.take([NC, H])
    nmax = A.take([NT, H])
    rsum = A.take([NT, H])
    xrow = A.take([O])
    fin = A.take([O])
    v = A.take([H, O])
    e = A.take([H, O])

    pT = [c["psum"][b][:, :].rearrange("p (c i) -> p c i", i=P) for b in range(2)]
    pW = c["psum"][2][:, 0:512].rearrange("p (h i) -> p h i", h=H)
    pH = c["psum"][2][:, 512:512 + P]
    pO = c["psum"][3][:, 0:512].rearrange("p (h i) -> p h i", h=H)

    d_h0 = sem("d_x_landed")
    d_h = sem("d_h_ready")
    d_wbc = sem("d_wbc")
    d_hc = sem("d_hc_copied")
    d_hps = sem("d_h_turned")
    d_hT = sem("d_hT_copied")
    d_small = sem("d_small_products")
    d_small_out = sem("d_small_products_read")
    d_nat = [sem(f"d_nat{b}_landed") for b in range(2)]
    d_turn = sem("d_adj_turned")
    d_zfree = sem("d_z_free")
    d_u = sem("d_u")
    d_l = sem("d_lrelu")
    d_z = sem("d_z_masked")
    d_s = sem("d_z_shifted")
    d_u2 = sem("d_step_max")
    d_e = sem("d_exp")
    d_comb = sem("d_combine")
    d_combe = sem("d_combine_exp")
    d_v = sem("d_final_sum")
    d_ve = sem("d_final_exp")
    d_f = sem("d_final_steps")
    d_fin = sem("d_final_ready")
    d_x = sem("d_xrow_landed")
    d_out = sem("d_out_stored")

    S1 = NT * NC
    COMB = 4
    FINAL = 4

    def dense(eng, program):
        go = eng.value_load(flag[0:1, 0:1], min_val=0, max_val=1)
        with eng.If(go > 0):
            program(eng)

    def dense_sync(sp):
        sp.dma_start(h, x_t).then_inc(d_h0, 16)
        sp.sem_inc(d_out, 16)
        with sp.Fori(0, NT) as j:
            with sp.Fori(0, NC // 2) as c:
                for b in range(2):
                    n = j * NC + c * 2 + b
                    sp.wait_ge(d_turn, n + 1)
                    sp.dma_start(nat[b].rearrange("p (c j) -> p c j", c=CH),
                                 adj_t[:, bass.ds((c * 2 + b) * CH, CH), bass.ds(j * P, P)]).then_inc(d_nat[b], 16)
        with sp.Fori(0, NT) as t:
            sp.wait_ge(d_fin, t + 1)
            sp.dma_start(xrow, x_t[:, t, :]).then_inc(d_x, 16)
            with sp.Fori(0, NC // 2) as g:
                for b in range(2):
                    n = t * NC + g * 2 + b + S1
                    sp.wait_ge(d_turn, n + 1)
                    sp.dma_start(nat[b], adj_t[:, t, bass.ds((g * 2 + b) * CH * P, CH * P)]).then_inc(d_nat[b], 16)
            sp.wait_ge(d_fin, t + 2)
            sp.dma_start(out_t[:, t, :], fin).then_inc(d_out, 16)
        sp.wait_ge(d_out, (NT + 1) * 16)

    def dense_tensor(pe):
        def turn_h(k):
            pe.wait_ge(d_hc, k + 1)
            pe.transpose(pH, hc, ident[:, :]).then_inc(d_hps, 1)
            pe.wait_ge(d_hT, k + 1)

        def spread_src():
            for hd in range(H):
                mm = pe.matmul(pW[:, hd, :], w_bc[:, hd, :], hT, start=True, stop=True, skip_group_check=True)
            return mm

        def turn_adj(n, b, cycle):
            pe.wait_ge(d_nat[b], (cycle + 1) * 16)
            pe.wait_ge(d_z, n + 1)
            for c in range(CH):
                mm = pe.transpose(pT[b][:, c, :], nat[b][:, c * P:(c + 1) * P], ident[:, :])
            mm.then_inc(d_turn, 1)

        pe.sem_inc(d_turn, 2)
        pe.wait_ge(d_wbc, 1)
        with pe.Fori(0, NT) as t:
            turn_h(t)
            spread_src()
            pe.matmul(pH[:, 0:2 * H], hT, wst[:, :], start=True, stop=True).then_inc(d_small, 1)
        with pe.Fori(0, NT) as j:
            with pe.Fori(0, NC // 2) as c:
                for b in range(2):
                    turn_adj(j * NC + c * 2 + b, b, j * (NC // 2) + c)
        with pe.Fori(0, NT) as t:
            turn_h(t + NT)
            pe.matmul(pW[:, :, :], hT, w_sb[:, :, :].rearrange("f h o -> f (h o)"),
                      start=True, stop=True).then_inc(d_small, 1)
        with pe.Fori(0, NT) as t:
            turn_h(t + 2 * NT)
            spread_src().then_inc(d_small, 1)
            pe.wait_ge(d_v, t + 1)
            for gg in range(NC // 2):
                for b in range(2):
                    g = gg * 2 + b
                    n = t * NC + g + S1
                    turn_adj(n, b, (t + NT) * (NC // 2) + gg)
                    pe.wait_ge(d_e, t * NC + g + 1)
                    for c in range(CH):
                        for hd in range(H):
                            mm = pe.matmul(pO[:, hd, :], z[:, hd, c, :], proj[:, g * CH + c, hd, :],
                                           start=(g == 0 and c == 0 and hd == 0), stop=(g == NC - 1 and c == CH - 1),
                                           skip_group_check=True)
                    mm.then_inc(d_zfree, 1)

    def dense_scalar(act):
        def copy_h(k, t):
            act.copy(hc, h[:, t, :]).then_inc(d_hc, 1)
            act.wait_ge(d_hps, k + 1)
            act.copy(hT, pH).then_inc(d_hT, 1)
            act.wait_ge(d_small, k + 1)
        act.wait_ge(d_h, NT + 1)
        with act.Fori(0, NT) as t:
            copy_h(t, t)
            act.copy(src_all[:, :, t, :], pW[:, :, :])
            act.copy(st[:, t, :], pH[:, 0:2 * H]).then_inc(d_small_out, 1)
        with act.Fori(0, NT) as j:
            with act.Fori(0, NC) as c:
                n = j * NC + c
                act.wait_ge(d_s, n + 1)
                for hd in range(H):
                    ins = act.activation(z[:, hd], z[:, hd], ACT.Exp, bias=nsmax[:, c, hd:hd + 1],
                                         accum_out=csum[:, c, hd:hd + 1])
                ins.then_inc(d_zfree, 1)
            act.wait_ge(d_comb, j * COMB + 2)
            act.activation(nsmax, nsmax, ACT.Exp).then_inc(d_combe, 1)
        with act.Fori(0, NT) as t:
            copy_h(t + NT, t)
            act.wait_ge(d_comb, NT * COMB + t + 2)
        with act.Fori(0, NT) as t:
            copy_h(t + 2 * NT, t)
            act.copy(src_row[:, :, :], pW[:, :, :]).then_inc(d_small_out, 1)
            with act.Fori(0, NC) as g:
                n = t * NC + g + S1
                act.wait_ge(d_s, n + 1)
                act.activation(z[:, :, :, :], z[:, :, :, :], ACT.Exp).then_inc(d_e, 1)
            act.wait_ge(d_v, t + 2)
            act.activation(e[:, :, :], v[:, :, :], ACT.Exp).then_inc(d_ve, 1)

    def dense_vector(dve):
        def scores(n, src, tgt, T):
            dve.wait_ge(d_zfree, n + 1)
            dve.tensor_tensor(z[:, :, :, :], src, tgt, ALU.add).then_inc(d_u, 1)
            dve.wait_ge(d_u, n + 1)
            dve.scalar_tensor_tensor(z[:, :, :, :], z[:, :, :, :], SLOPE, z[:, :, :, :],
                                     ALU.mult, ALU.max).then_inc(d_l, 1)
            dve.wait_ge(d_l, n + 1)
            dve.wait_ge(d_turn, n + 3)
            dve.tensor_tensor(z[:, :, :, :], z[:, :, :, :],
                              T[:, :, :].rearrange("p (g c) i -> p g c i", g=1).to_broadcast([P, H, CH, P]),
                              ALU.add).then_inc(d_z, 1)
            dve.wait_ge(d_z, n + 3)

        dve.wait_ge(d_h0, 16)
        with dve.Fori(0, NT) as t:
            dve.tensor_scalar(h[:, t, :], h[:, t, :], rstd[:, bass.ds(t, 1)], nmr[:, bass.ds(t, 1)],
                              ALU.mult, ALU.add).then_inc(d_h, 1)
        dve.wait_ge(d_h, NT)
        dve.tensor_scalar(h, h, 0.0, None, ALU.max).then_inc(d_h, 1)
        dve.sem_inc(d_z, 2)
        dve.sem_inc(d_zfree, 1)
        dve.sem_inc(d_v, 1)
        dve.sem_inc(d_fin, 1)
        for hd in range(H):
            ins = dve.tensor_copy(w_bc[:, hd, :], wst[:, hd:hd + 1].to_broadcast([P, P]))
        ins.then_inc(d_wbc, 1)
        dve.wait_ge(d_small_out, NT)
        with dve.Fori(0, NT) as j:
            with dve.Fori(0, NC // 2) as cc:
                for b in range(2):
                    c = cc * 2 + b
                    n = j * NC + c
                    scores(n, src_all[:, :, bass.ds(c * CH, CH), :],
                           st[:, j, H:2 * H].unsqueeze(2).unsqueeze(3).to_broadcast([P, H, CH, P]), pT[b])
                    dve.tensor_reduce(smax, z[:, :, :, :].rearrange("p h c i -> p h (c i)"), AX.X,
                                      ALU.max).then_inc(d_u2, 1)
                    dve.wait_ge(d_u2, n + 1)
                    dve.tensor_scalar(nsmax[:, c, :], smax, -1.0, None, ALU.mult).then_inc(d_s, 1)
            dve.wait_ge(d_zfree, j * NC + NC + 1)
            dve.tensor_reduce(nmax[:, j, :], nsmax.rearrange("p c h -> p h c"), AX.X,
                              ALU.min).then_inc(d_comb, 1)
            dve.wait_ge(d_comb, j * COMB + 1)
            dve.scalar_tensor_tensor(nsmax, nsmax, -1.0,
                                     nmax[:, j, :].unsqueeze(1).to_broadcast([P, NC, H]),
                                     ALU.mult, ALU.add).then_inc(d_comb, 1)
            dve.wait_ge(d_combe, j + 1)
            dve.tensor_tensor(csum[:, :, :], csum[:, :, :], nsmax, ALU.mult).then_inc(d_comb, 1)
            dve.wait_ge(d_comb, j * COMB + 3)
            dve.tensor_reduce(rsum[:, j, :], csum[:, :, :].rearrange("p c h -> p h c"), AX.X,
                              ALU.add).then_inc(d_comb, 1)
        dve.wait_ge(d_comb, NT * COMB)
        dve.reciprocal(rsum, rsum).then_inc(d_comb, 1)
        dve.wait_ge(d_comb, NT * COMB + 1)
        with dve.Fori(0, NT) as t:
            dve.wait_ge(d_small, t + NT + 1)
            dve.tensor_tensor(proj[:, t], pW[:, :, :], rsum[:, t, :].unsqueeze(2).to_broadcast([P, H, O]),
                              ALU.mult).then_inc(d_comb, 1)
        with dve.Fori(0, NT) as t:
            dve.wait_ge(d_small_out, t + NT + 1)
            for gg in range(NC // 2):
                for b in range(2):
                    n = t * NC + gg * 2 + b + S1
                    tiles = slice((gg * 2 + b) * CH, (gg * 2 + b + 1) * CH)
                    scores(n, src_row[:, :, :].unsqueeze(2).to_broadcast([P, H, CH, P]),
                           st[:, tiles, H:2 * H].rearrange("p c h -> p h c").unsqueeze(3).to_broadcast([P, H, CH, P]),
                           pT[b])
                    dve.tensor_tensor(z[:, :, :, :], z[:, :, :, :],
                                      nmax[:, tiles, :].rearrange("p c h -> p h c").unsqueeze(3).to_broadcast([P, H, CH, P]),
                                      ALU.add).then_inc(d_s, 1)
            dve.wait_ge(d_zfree, (t + 1) * NC + S1 + 1)
            dve.tensor_tensor(v[:, :, :], pO[:, :, :], h[:, t, :].unsqueeze(1).to_broadcast([P, H, O]),
                              ALU.add).then_inc(d_v, 1)
            dve.wait_ge(d_ve, t + 1)
            dve.tensor_scalar(e[:, :, :], e[:, :, :], 1.0, -1.0, ALU.min, ALU.add).then_inc(d_f, 1)
            dve.wait_ge(d_f, t * FINAL + 1)
            dve.tensor_tensor(v[:, :, :], v[:, :, :], e[:, :, :], ALU.max).then_inc(d_f, 1)
            dve.wait_ge(d_f, t * FINAL + 2)
            dve.tensor_tensor(v[:, 0:2, :], v[:, 0:2, :], v[:, 2:4, :], ALU.add).then_inc(d_f, 1)
            dve.wait_ge(d_f, t * FINAL + 3)
            dve.tensor_tensor(v[:, 0, :], v[:, 0, :], v[:, 1, :], ALU.add).then_inc(d_f, 1)
            dve.wait_ge(d_f, t * FINAL + 4)
            dve.wait_ge(d_x, (t + 1) * 16)
            dve.wait_ge(d_out, (t + 1) * 16)
            dve.scalar_tensor_tensor(fin, v[:, 0, :], 1.0 / H, xrow, ALU.mult, ALU.add).then_inc(d_fin, 1)

    with nc.Block() as block:
        @block.sync
        def _(sp):
            dense(sp, dense_sync)

        @block.tensor
        def _(pe):
            dense(pe, dense_tensor)

        @block.scalar
        def _(act):
            dense(act, dense_scalar)

        @block.vector
        def _(dve):
            dense(dve, dense_vector)


_INS = ["x", "adj", "L0_gnn_W", "L0_gnn_a_src", "L0_gnn_a_tgt"]


def kernel(**inputs):
    import numpy as np
    import concourse.bacc as bacc
    from concourse.bass_utils import run_bass_kernel_spmd

    nc = bacc.Bacc("TRN2", target_bir_lowering=False, num_devices=1)
    arrays, args = {}, []
    for name in _INS:
        a = np.ascontiguousarray(inputs[name])
        arrays[f"in_{name}"] = a
        args.append(nc.dram_tensor(f"in_{name}", a.shape, mybir.dt.from_np(a.dtype), kind="ExternalInput").ap())
    shape = inputs["x"].shape
    args.append(nc.dram_tensor("out", shape, F32, kind="ExternalOutput").ap())
    gat_kernel(nc, *args)
    r = run_bass_kernel_spmd(nc, [arrays], core_ids=[0])
    return r.results[0]["out"]
```

```python
from contextlib import ExitStack

import concourse.bass as bass
from concourse import mybir

P = 128
F32 = mybir.dt.float32
I32 = mybir.dt.int32
U32 = mybir.dt.uint32
ALU = mybir.AluOpType
ACT = mybir.ActivationFunctionType
AX = mybir.AxisListType
EPS = 1e-5
SLOPE = 0.2

KAPPA = 2.0 ** -5
GAP = 16.5 / KAPPA
UNDERFLOW = 105.0
ROUNDING = 2.0 ** -22


class Arena:

    def __init__(self, tensor, start=0):
        self.tensor, self.at = tensor, start

    def take(self, dims, dt=F32):
        words = 1
        for d in dims:
            words *= d
        assert self.at + words <= self.tensor.shape[1], (self.at, words)
        v = self.tensor[:, self.at:self.at + words]
        self.at += words
        if dt != F32:
            v = v.bitcast(dt)
        names = "abcd"[:len(dims)]
        if len(dims) > 1:
            v = v.rearrange("p (" + " ".join(names) + ") -> p " + " ".join(names),
                            **{n: d for n, d in zip(names, dims)})
        return v


def gat_kernel(nc, x, adj, W, a_src, a_tgt, out):
    N, F = x.shape
    H, _, O = W.shape
    NT = N // P
    CH = 8
    NC = NT // CH
    assert F == P and O == P and H * O == 512 and NT % (2 * CH) == 0

    with ExitStack() as ctx:
        def sb(name, shape, dt=F32):
            return ctx.enter_context(nc.sbuf_tensor(name, shape, dt))

        c = dict(N=N, F=F, H=H, O=O, NT=NT, CH=CH, NC=NC)
        c["w_sb"] = sb("w_sb", [P, H, O])
        c["wst"] = sb("wst", [P, 2 * H])
        c["ident"] = sb("ident", [P, P])
        c["ones"] = sb("ones", [P, P])
        c["mean"] = sb("mean", [P, NT])
        c["rstd"] = sb("rstd", [P, NT])
        c["nmr"] = sb("nmr", [P, NT])
        c["flag"] = sb("flag", [1, 1], I32)
        c["arena"] = sb("arena", [P, 52150])
        c["x_t"] = x.rearrange("(t p) f -> p t f", p=P)
        c["out_t"] = out.rearrange("(t p) f -> p t f", p=P)
        c["adj_t"] = adj.rearrange("(t p) j -> p t j", p=P)
        c["psum"] = [ctx.enter_context(nc.psum_tensor(f"ps{b}", [P, 1024], F32)) for b in range(4)]

        peaked_path(nc, ctx, c, W, a_src, a_tgt)
        dense_path(nc, ctx, c)


def peaked_path(nc, ctx, c, W, a_src, a_tgt):
    N, F, H, O, NT = (c[k] for k in ("N", "F", "H", "O", "NT"))
    w_sb, wst, ident, ones, mean, rstd, nmr, flag = (
        c[k] for k in ("w_sb", "wst", "ident", "ones", "mean", "rstd", "nmr", "flag"))
    x_t, out_t, adj_t = (c[k] for k in ("x_t", "out_t", "adj_t"))
    NP = 4
    PT = NT // NP
    G = 8
    RT = NT // G
    RC = RT * P
    NS = 4
    DEPTH = 3

    def sem(name):
        return ctx.enter_context(nc.semaphore(name))

    sums = nc.dram_tensor("sums", [N + P, F], F32).ap()
    sums_t = sums.rearrange("(t p) f -> p t f", p=P)

    A = Arena(c["arena"])
    h = A.take([NT, F])
    S0 = A.at
    strips = A.take([NS, NT, P])
    half_max = A.take([NT // 2, P])
    rowmax = A.take([RT, P])
    place = A.take([RC])
    range_at = A.take([G])
    dummy = A.take([1])
    earlier = A.take([P])
    cert = A.take([NS, G + 1])
    hist = A.take([NT, G + 1])
    cmx = A.take([2])
    in_range = A.take([2])
    base = A.take([2])
    junk8 = A.take([2, G])
    junk = A.take([P])
    idx = A.take([2])
    same = A.take([P])
    dup = A.take([2])
    target = A.take([NS, 1], U32)
    rows = A.take([NS, F])
    zero = A.take([F])
    small = A.take([4])
    bad = A.take([4])
    tot = A.take([NT])
    wsq = A.take([2 * H])
    flag_f = A.take([1])
    a_bc = A.take([2, H, O])
    a_w = A.take([2, H, O])
    stats = A.take([NT, 6])
    half = A.take([NT])
    var = A.take([NT])
    D = Arena(c["arena"], S0)
    BT = 4
    agg = D.take([NT, F])
    stage = D.take([2, RC])
    x_rows = D.take([2, RT, F])
    v = D.take([2 * RT // BT, BT, H, O])
    e = D.take([2, 2, H, O])
    s2 = D.take([2, BT, 2, O])
    s1 = D.take([2 * RT // BT, BT, O])
    osb = D.take([2, RT, O])
    assert D.at <= S0 + NS * NT * P

    turned_ps = [c["psum"][b][:, :].rearrange("p (t i) -> p t i", i=P) for b in range(2)]
    cells_ps = c["psum"][2]
    idx_ps = c["psum"][3][:, 0:P]
    sum_ps = c["psum"][3][:, 512:512 + F]
    proj_ps = [c["psum"][b] for b in range(2)]
    agg_ps = [c["psum"][2 + b] for b in range(2)]

    s_w = sem("weights_landed")
    s_x = [sem(f"x{i}_landed") for i in range(NP)]
    s_ones = sem("ones_set")
    s_ident = sem("ident_set")
    s_zero = sem("zero_set")
    s_const = sem("constants_set")
    s_cleared = sem("sums_cleared")
    s_set = sem("setup_vector")
    s_sqrt = sem("setup_sqrt")
    s_stat = sem("layernorm_statistics")
    f_in = [sem(f"strip_piece{i}_landed") for i in range(NS * NP)]
    f_turn = sem("range_turned")
    f_exp = sem("range_exped")
    f_kept = sem("cert_kept")
    f_h = sem("h_tile")
    f_pairs = sem("pairs_max")
    f_max = sem("strip_max")
    f_mt = sem("maxima_turned")
    f_mx = sem("column_max")
    f_nb = sem("bias_ready")
    f_up = sem("place_in_range")
    f_base = sem("range_found")
    f_idx = sem("row_found")
    f_idt = sem("rows_found_turned")
    f_same = sem("same_rows_found")
    f_dup = sem("duplicates_counted")
    f_target = sem("target_rows")
    f_sum = sem("same_rows_summed")
    f_rows = sem("summands_ready")
    f_added = sem("summands_added")
    w_sync = sem("waited_sync")
    w_pool = sem("waited_gpsimd")
    t_agg = [sem(f"sums{k}_landed") for k in range(G)]
    t_turn = sem("tail_sums_turned")
    t_stage = sem("tail_sums_staged")
    t_x = [sem(f"x_rows{b}_landed") for b in range(2)]
    t_p = sem("tail_projected")
    t_v = sem("tail_v")
    t_e = sem("tail_exp")
    t_u = sem("tail_exp_below_one")
    t_m = sem("tail_elu")
    t_s2 = sem("tail_two_heads")
    t_s1 = sem("tail_head_sum")
    t_o = sem("tail_rows")
    t_out = [sem(f"tail_stored{b}") for b in range(2)]
    g_d = sem("check_vector")
    g_n = sem("check_norms")
    g_b = sem("check_turned")

    def strips_of(engine, body):
        for u in range(NS):
            body(u, u, u > 0, True, True)
        with engine.Fori(1, NT // NS - 1) as g:
            for u in range(NS):
                body(g * NS + u, u, True, True, True)
        for u in range(NS):
            body(NT - NS + u, u, True, u < NS - 1, u < NS - 2)

    def added_before(engine, s):
        if not isinstance(s, int) or s > 0:
            engine.wait_ge(f_added, s * 16)

    def tail_of(engine, body):
        with engine.Fori(0, G // 2 - 1) as kk:
            body(kk, True)
        body(G // 2 - 1, False)

    def landed(s, u):
        return (s - u) * (16 // NS) + 16

    in_order = (0, 2, 1, 3)
    NB = 2 * RT // BT
    STORED = 16 * (RT // BT)
    CHECKS = 20

    with nc.Block() as block:
        @block.sync
        def _(sp):
            sp.sem_inc(f_turn, NS * G)
            def strip(s, u):
                for n, i in enumerate(in_order):
                    if n >= DEPTH:
                        sp.wait_ge(f_in[u * NP + in_order[n - DEPTH]], landed(s, u))
                    elif not (isinstance(s, int) and s == 0):
                        sp.wait_ge(f_in[(u - 1) % NS * NP + in_order[n - DEPTH]], landed(s - 1, (u - 1) % NS))
                    sp.sem_inc(w_sync, 1)
                    sp.wait_ge(f_turn, s * G + (i + 1) * (G // NP))
                    sp.dma_start(strips[:, u, i * PT:(i + 1) * PT, :],
                                 adj_t[:, i * PT:(i + 1) * PT, bass.ds(s * P, P)]).then_inc(f_in[u * NP + i], 16)
            strip(0, 0)
            sp.dma_start(w_sb[:, :, :], W.rearrange("h f o -> f h o")).then_inc(s_w, 16)
            sp.dma_start(a_bc[:, 0], a_src.partition_broadcast(P)).then_inc(s_w, 16)
            sp.dma_start(a_bc[:, 1], a_tgt.partition_broadcast(P)).then_inc(s_w, 16)
            for i in range(NP):
                sp.dma_start(h[:, i * PT:(i + 1) * PT, :], x_t[:, i * PT:(i + 1) * PT, :]).then_inc(s_x[i], 16)
            strip(1, 1)
            sp.wait_ge(s_zero, 1)
            sp.dma_start(sums_t, zero.unsqueeze(1).to_broadcast([P, NT + 1, F])).then_inc(s_cleared, 16)
            for u in range(2, NS):
                strip(u, u)
            with sp.Fori(1, NT // NS) as g:
                for u in range(NS):
                    strip(g * NS + u, u)
            sp.wait_ge(f_turn, (NT + NS) * G)
            for q in range(2):
                sp.dma_start(x_rows[:, q], x_t[:, q * RT:(q + 1) * RT, :]).then_inc(t_x[q], 16)
            sp.wait_ge(f_added, NT * 16)
            for k in range(G):
                sp.dma_start(agg[:, k * RT:(k + 1) * RT, :], sums_t[:, k * RT:(k + 1) * RT, :]).then_inc(t_agg[k], 16)
            def tail(kk, more):
                for q in range(2):
                    for b in range(RT // BT):
                        sp.wait_ge(t_o, (kk * 2 + q) * (RT // BT) + b + 1)
                        sp.dma_start(out_t[:, bass.ds((kk * 2 + q) * RT + b * BT, BT), :],
                                     osb[:, q, b * BT:(b + 1) * BT]).then_inc(t_out[q], 16)
                    if more:
                        sp.dma_start(x_rows[:, q], x_t[:, bass.ds((kk * 2 + q + 2) * RT, RT), :]).then_inc(t_x[q], 16)
            tail_of(sp, tail)
            for q in range(2):
                sp.wait_ge(t_out[q], STORED * (G // 2 + 1))

        @block.gpsimd
        def _(pool):
            pool.memset(zero, 0.0).then_inc(s_zero, 1)
            pool.memset(ones[:, :], 1.0).then_inc(s_ones, 1)
            pool.wait_ge(s_ones, 1)
            pool.affine_select(ident[:, :], ones[:, :], pattern=[[-1, P]], compare_op=ALU.is_equal,
                               fill=0.0, base=0, channel_multiplier=1).then_inc(s_ident, 1)
            pool.iota(place, [[1, RC]], 0, 0, allow_small_or_imprecise_dtypes=True)
            pool.iota(range_at, [[RC, G]], 0, 0, allow_small_or_imprecise_dtypes=True)
            pool.iota(dummy, [[0, 1]], N, 1, allow_small_or_imprecise_dtypes=True)
            pool.iota(junk, [[0, P]], N, 1, allow_small_or_imprecise_dtypes=True).then_inc(s_const, 1)
            pool.wait_ge(s_const, 1)
            pool.affine_select(earlier, junk, pattern=[[-1, P]], compare_op=ALU.is_gt,
                               fill=0.0, base=0, channel_multiplier=1).then_inc(s_const, 1)
            pool.sem_inc(f_kept, NS)
            pool.sem_inc(t_s1, 2)
            pool.sem_inc(t_out[0], STORED)
            pool.sem_inc(t_out[1], STORED)

            def former(s, u):
                pool.wait_ge(f_exp, s * G + 2)
                pool.tensor_copy(hist[:, bass.ds(s - 1, 1), :], cert[:, u, :].unsqueeze(1)).then_inc(f_kept, 1)
                pool.wait_ge(f_rows, s + 1)
                pool.wait_ge(f_target, s + 1)
                added_before(pool, s - 1)
                pool.sem_inc(w_pool, 1)
                pool.indirect_dma_start(sums, bass.IndirectOffsetOnAxis(target[:, u, :], 0), rows[:, u, :], None,
                                        compute_op=ALU.add).then_inc(f_added, 16)

            def strip(s, u, has_former, has_next, has_next_but_one):
                if has_former:
                    former(s, (u - 1) % NS)
            pool.wait_ge(s_cleared, 16)
            strips_of(pool, strip)
            former(NT, NS - 1)
            def tail(kk, more):
                for b in range(NB):
                    n = kk * NB + b
                    pool.wait_ge(t_m, (n + 1) * (BT // 2) + 2)
                    pool.wait_ge(t_s1, n + 1)
                    pool.tensor_tensor(s2[:, b % 2], v[:, b, :, 0:2, :], v[:, b, :, 2:4, :], ALU.add).then_inc(t_s2, 1)
                    pool.wait_ge(t_s2, n + NB + 1)
                    pool.tensor_tensor(s1[:, b], s2[:, b % 2, :, 0, :], s2[:, b % 2, :, 1, :], ALU.add).then_inc(t_s1, 1)
            tail_of(pool, tail)

        @block.tensor
        def _(pe):
            def turn_maxima(s):
                pe.wait_ge(f_max, s + 1)
                pe.wait_ge(f_up, s + 1)
                for u in range(RT):
                    mm = pe.transpose(cells_ps[:, u * P:(u + 1) * P], rowmax[:, u, :], ident[:, :])
                mm.then_inc(f_mt, 1)

            def turn_idx(s, q):
                pe.wait_ge(f_idx, s)
                pe.transpose(idx_ps, idx[:, q:q + 1].to_broadcast([P, P]), ident[:, :]).then_inc(f_idt, 1)

            def sum_same(s):
                pe.wait_ge(f_same, s)
                pe.wait_ge(f_h, s)
                pe.wait_ge(f_rows, s)
                pe.matmul(sum_ps, same, h[:, bass.ds(s - 1, 1), :].rearrange("p t f -> p (t f)"),
                          start=True, stop=True).then_inc(f_sum, 1)

            def strip(s, u, has_former, has_next, has_next_but_one):
                for r in range(G):
                    pe.wait_ge(f_exp, s * G + r + 1)
                    if r % (G // NP) == 0:
                        pe.wait_ge(f_in[u * NP + r // (G // NP)], landed(s, u))
                    for m in range(RT):
                        mm = pe.transpose(turned_ps[r % 2][:, m, :], strips[:, u, r * RT + m, :], ident[:, :])
                    mm.then_inc(f_turn, 1)
                    if has_former and r == 5:
                        turn_idx(s, (u + 1) % 2)
                if has_next:
                    turn_maxima(s + 1)
                if has_former:
                    sum_same(s)

            def turn_sums(k):
                pe.wait_ge(t_agg[k], 16)
                for m in range(RT):
                    mm = pe.transpose(agg_ps[k % 2][:, m * P:(m + 1) * P], agg[:, k * RT + m, :], ident[:, :])
                mm.then_inc(t_turn, 1)

            def tail(k):
                pe.wait_ge(t_stage, k + 1)
                for m in range(0, RT, 2):
                    pe.wait_ge(t_v, (k * RT + m) // 2 + 1)
                    for i in range(2):
                        mm = pe.matmul(proj_ps[m // 2 % 2][:, i * H * O:(i + 1) * H * O],
                                       stage[:, k % 2, (m + i) * P:(m + i + 1) * P],
                                       w_sb[:, :, :].rearrange("f h o -> f (h o)"), start=True, stop=True)
                    mm.then_inc(t_p, 1)
                if k + 2 < G:
                    turn_sums(k + 2)

            pe.sem_inc(f_sum, 1)
            pe.wait_ge(s_ident, 1)
            turn_maxima(0)
            strips_of(pe, strip)
            turn_idx(NT, 1)
            sum_same(NT)
            pe.wait_ge(f_exp, NT * G + 2)
            pe.wait_ge(g_d, 1)
            pe.matmul(proj_ps[1][:, 512:512 + 2 * H], ones[:, :], wsq[:, :], start=True, stop=True).then_inc(g_n, 1)
            pe.wait_ge(g_d, CHECKS - 2)
            pe.transpose(proj_ps[1][0:1, 0:P], bad[:, 0:1], ident[:, :]).then_inc(g_b, 1)
            pe.wait_ge(f_rows, NT + 1)
            turn_sums(0)
            turn_sums(1)
            pe.wait_ge(g_d, CHECKS)
            for k in range(G):
                tail(k)

        @block.scalar
        def _(act):
            def h_tile(s):
                tile = h[:, bass.ds(s, 1), :].rearrange("p t f -> p (t f)")
                act.activation(tile, tile, ACT.Relu, scale=rstd[:, bass.ds(s, 1)],
                               bias=nmr[:, bass.ds(s, 1)]).then_inc(f_h, 1)

            def strip(s, u, has_former, has_next, has_next_but_one):
                act.wait_ge(f_nb, s + 1)
                act.wait_ge(f_kept, s + 1)
                for r in range(G):
                    act.wait_ge(f_turn, s * G + r + 1 + NS * G)
                    act.activation(turned_ps[r % 2], turned_ps[r % 2], ACT.Exp, scale=KAPPA, bias=cert[:, u, G:G + 1],
                                   accum_out=cert[:, u, r:r + 1]).then_inc(f_exp, 1)
                if not has_former:
                    act.wait_ge(s_set, 4)
                    act.activation(half[:, :], var[:, :], ACT.Sqrt).then_inc(s_sqrt, 1)
                    act.wait_ge(s_stat, 4)
                if has_former:
                    copy_sum(s, (u - 1) % NS)
                h_tile(s)

            def copy_sum(s, u):
                act.wait_ge(f_sum, s + 1)
                added_before(act, s - NS)
                act.copy(rows[:, u, :], sum_ps).then_inc(f_rows, 1)

            def stage_sums(k, q):
                act.wait_ge(t_turn, k + 1)
                act.copy(stage[:, q, :], agg_ps[q][:, :]).then_inc(t_stage, 1)

            def tail(kk, more):
                for w in range(RT):
                    n = kk * RT + w
                    act.wait_ge(t_v, n + 3)
                    act.wait_ge(t_m, n + 1)
                    act.activation(e[:, w % 2], v[:, 2 * w // BT, 2 * w % BT:2 * w % BT + 2], ACT.Exp).then_inc(t_e, 1)
                    act.wait_ge(t_e, n + 1)
                    act.activation(e[:, w % 2], e[:, w % 2], ACT.Relu, scale=-1.0, bias=1.0).then_inc(t_u, 1)
                    if more and w % (RT // 2) == RT // 2 - 1:
                        stage_sums(kk * 2 + w // (RT // 2) + 2, w // (RT // 2))

            act.sem_inc(f_exp, 2)
            act.sem_inc(f_rows, 1)
            strips_of(act, strip)
            copy_sum(NT, NS - 1)
            stage_sums(0, 0)
            stage_sums(1, 1)
            tail_of(act, tail)

        @block.vector
        def _(dve):
            def strip_max(s, u, step):
                if step < 2:
                    for i in (step, step + 2):
                        dve.wait_ge(f_in[u * NP + i], landed(s, u))
                    t = slice(step * NT // 4, (step + 1) * NT // 4)
                    dve.tensor_tensor(half_max[:, t, :], strips[:, u, t, :],
                                      strips[:, u, t.start + NT // 2:t.stop + NT // 2, :], ALU.max).then_inc(f_pairs, 1)
                elif step == 2:
                    dve.wait_ge(f_pairs, s * 3 + 2)
                    dve.tensor_tensor(half_max[:, 0:NT // 4, :], half_max[:, 0:NT // 4, :],
                                      half_max[:, NT // 4:NT // 2, :], ALU.max).then_inc(f_pairs, 1)
                else:
                    dve.wait_ge(f_pairs, s * 3 + 3)
                    dve.tensor_tensor(rowmax[:, :, :], half_max[:, 0:RT, :], half_max[:, RT:2 * RT, :],
                                      ALU.max).then_inc(f_max, 1)

            def column_max(s, u):
                q = u % 2
                dve.wait_ge(f_mt, s + 1)
                dve.tensor_reduce(cmx[:, q:q + 1], cells_ps[:, :], AX.X, ALU.max).then_inc(f_mx, 1)
                dve.wait_ge(f_mx, s + 1)
                dve.wait_ge(f_kept, s + 1)
                dve.tensor_scalar(cert[:, u, G:G + 1], cmx[:, q:q + 1], -KAPPA, None, ALU.mult).then_inc(f_nb, 1)
                dve.scalar_tensor_tensor(cells_ps[:, :], cells_ps[:, :], cmx[:, q:q + 1], place,
                                         ALU.is_equal, ALU.mult, accum_out=in_range[:, q:q + 1]).then_inc(f_up, 1)

            def find_row(s, u):
                q = u % 2
                dve.wait_ge(f_exp, s * G + 2)
                dve.scalar_tensor_tensor(junk8[:, q, :], cert[:, u, 0:G], 0.5, range_at,
                                         ALU.is_ge, ALU.mult, accum_out=base[:, q:q + 1]).then_inc(f_base, 1)
                dve.wait_ge(f_base, s)
                dve.wait_ge(f_up, s + 1)
                dve.wait_ge(f_target, s)
                dve.tensor_scalar(idx[:, q:q + 1], base[:, q:q + 1], in_range[:, q:q + 1], N - 1.0,
                                  ALU.add, ALU.min).then_inc(f_idx, 1)

            def find_same(s, u):
                q = u % 2
                dve.wait_ge(f_idt, s)
                dve.wait_ge(f_sum, s)
                dve.tensor_scalar(same, idx_ps, idx[:, q:q + 1], None, ALU.is_equal).then_inc(f_same, 1)
                dve.scalar_tensor_tensor(junk, idx_ps, idx[:, q:q + 1], earlier,
                                         ALU.is_equal, ALU.mult, accum_out=dup[:, q:q + 1]).then_inc(f_dup, 1)
                dve.wait_ge(f_dup, s)
                added_before(dve, s - NS)
                dve.tensor_scalar(target[:, u, :], dup[:, q:q + 1], dummy, idx[:, q:q + 1],
                                  ALU.min, ALU.max).then_inc(f_target, 1)

            def strip(s, u, has_former, has_next, has_next_but_one):
                if has_next:
                    strip_max(s + 1, (u + 1) % NS, 1)
                if has_former:
                    find_row(s, (u - 1) % NS)
                if has_next:
                    strip_max(s + 1, (u + 1) % NS, 2)
                    strip_max(s + 1, (u + 1) % NS, 3)
                if has_former:
                    find_same(s, (u - 1) % NS)
                if has_next:
                    if has_next_but_one:
                        dve.wait_ge(f_max, s + 2)
                        strip_max(s + 2, (u + 2) % NS, 0)
                    column_max(s + 1, (u + 1) % NS)

            def tail(kk, more, first=False):
                def elu(w):
                    dve.wait_ge(t_u, kk * RT + w + 1)
                    at = 2 * (w % RT)
                    tiles = v[:, at // BT, at % BT:at % BT + 2].rearrange("p t h o -> p (t h o)")
                    dve.scalar_tensor_tensor(tiles, e[:, w % 2].rearrange("p t h o -> p (t h o)"), -1.0, tiles,
                                             ALU.mult, ALU.max).then_inc(t_m, 1)
                def finish(m):
                    back = 1 if m < 0 else 0
                    b = m // BT + back * NB
                    q, at = b * BT // RT, b * BT % RT
                    dve.wait_ge(t_s1, (kk - back) * NB + b + 3)
                    dve.wait_ge(t_x[q], (kk - back + 1) * 16)
                    dve.wait_ge(t_out[q], (kk - back + 1) * STORED)
                    dve.scalar_tensor_tensor(osb[:, q, at:at + BT, :], s1[:, b], 1.0 / H,
                                             x_rows[:, q, at:at + BT, :], ALU.mult, ALU.add).then_inc(t_o, 1)
                for w in range(RT):
                    n = kk * RT + w
                    m = 2 * w
                    if m % BT == 0 and not (first and m < 3 * BT):
                        finish(m - 3 * BT)
                    dve.wait_ge(t_p, n + 1)
                    if m % BT == 0:
                        dve.wait_ge(t_s2, kk * NB + m // BT + 1)
                    dve.tensor_tensor(v[:, m // BT, m % BT:m % BT + 2],
                                      h[:, bass.ds(2 * n, 2), :].unsqueeze(2).to_broadcast([P, 2, H, O]),
                                      proj_ps[w % 2].rearrange("p (t h o) -> p t h o", t=2, h=H), ALU.add).then_inc(t_v, 1)
                    if w > 1 or not first:
                        elu(w - 2)
                if not more:
                    elu(RT - 2)
                    elu(RT - 1)
                    for b in range(NB - 3, NB):
                        finish(b * BT)

            dve.sem_inc(f_up, 1)
            dve.sem_inc(f_target, 1)
            dve.sem_inc(t_v, 2)
            dve.sem_inc(t_m, 2)
            dve.sem_inc(t_s2, NB)
            dve.wait_ge(s_const, 2)
            for step in range(4):
                strip_max(0, 0, step)
            dve.wait_ge(f_max, 1)
            column_max(0, 0)
            dve.wait_ge(s_w, 48)
            for k in range(2):
                ins = dve.tensor_tensor(a_w[:, k], w_sb[:, :, :], a_bc[:, k], ALU.mult)
            ins.then_inc(s_set, 1)
            dve.wait_ge(s_set, 1)
            dve.tensor_reduce(wst[:, :].rearrange("p (k h) -> p k h", k=2), a_w, AX.X, ALU.add).then_inc(s_set, 1)
            dve.wait_ge(s_set, 2)
            dve.tensor_tensor(wsq, wst[:, :], wst[:, :], ALU.mult).then_inc(g_d, 1)
            for i in range(NP):
                dve.wait_ge(s_x[i], 16)
                for t in range(i * PT, (i + 1) * PT):
                    ins = dve.bn_stats(stats[:, t, :], h[:, t, :])
            ins.then_inc(s_set, 1)
            dve.wait_ge(s_set, 3)
            me, qe, mo, qo = (stats[:, :, i] for i in (1, 2, 4, 5))
            dve.tensor_tensor(mean[:, :], me, mo, ALU.add)
            dve.tensor_tensor(half, me, mo, ALU.subtract)
            dve.tensor_tensor(var, qe, qo, ALU.add).then_inc(s_stat, 1)
            dve.wait_ge(s_stat, 1)
            dve.tensor_scalar(mean[:, :], mean[:, :], 0.5, None, ALU.mult)
            dve.tensor_scalar(var, var, 1.0 / F, EPS, ALU.mult, ALU.add)
            dve.scalar_tensor_tensor(half, half, 0.25, half, ALU.mult, ALU.mult).then_inc(s_stat, 1)
            dve.wait_ge(s_stat, 2)
            dve.tensor_tensor(var, var, half, ALU.add).then_inc(s_set, 1)
            dve.wait_ge(s_sqrt, 1)
            dve.reciprocal(rstd[:, :], half).then_inc(s_stat, 1)
            dve.wait_ge(s_stat, 3)
            dve.scalar_tensor_tensor(nmr[:, :], mean[:, :], -1.0, rstd[:, :], ALU.mult, ALU.mult).then_inc(s_stat, 1)

            strip_max(1, 1, 0)
            strips_of(dve, strip)
            find_row(NT, NS - 1)
            find_same(NT, NS - 1)

            dve.wait_ge(f_kept, NT + NS)
            lim, neg, nrm = small[:, 0:1], small[:, 1:2], small[:, 2:3]
            count = [1]

            def done(ins):
                ins.then_inc(g_d, 1)
                count[0] += 1
                dve.wait_ge(g_d, count[0])
            done(dve.tensor_reduce(tot, hist[:, :, 0:G], AX.X, ALU.add))
            done(dve.tensor_scalar(tot, tot, 1.0, None, ALU.not_equal))
            done(dve.tensor_scalar(half, nmr[:, :], 0.0, 0.0, ALU.mult, ALU.not_equal))
            done(dve.tensor_tensor(tot, tot, half, ALU.max))
            done(dve.tensor_reduce(bad[:, 1:2], tot, AX.X, ALU.max))
            done(dve.tensor_reduce(lim, hist[:, :, G], AX.X, ALU.max))
            done(dve.tensor_reduce(neg, hist[:, :, G], AX.X, ALU.min))
            done(dve.tensor_scalar(neg, neg, -1.0, None, ALU.mult))
            done(dve.tensor_tensor(lim, lim, neg, ALU.max))
            done(dve.tensor_scalar(lim, lim, -ROUNDING / KAPPA, GAP - UNDERFLOW, ALU.mult, ALU.add))
            done(dve.tensor_scalar(lim, lim, 0.0, None, ALU.max))
            done(dve.tensor_tensor(lim, lim, lim, ALU.mult))
            dve.wait_ge(g_n, 1)
            done(dve.tensor_reduce(nrm, proj_ps[1][:, 512:512 + 2 * H], AX.X, ALU.max))
            done(dve.tensor_scalar(nrm, nrm, 4.0 * F * 1.02, None, ALU.mult))
            done(dve.tensor_tensor(nrm, nrm, lim, ALU.is_lt))
            done(dve.tensor_scalar(bad[:, 2:3], nrm, -1.0, 1.0, ALU.mult, ALU.add))
            done(dve.tensor_tensor(bad[:, 0:1], bad[:, 1:2], bad[:, 2:3], ALU.max))
            dve.wait_ge(g_b, 1)
            done(dve.tensor_reduce(flag_f[0:1, 0:1], proj_ps[1][0:1, 0:P], AX.X, ALU.max))
            done(dve.tensor_copy(flag[:, :], flag_f[0:1, 0:1]))
            assert count[0] == CHECKS
            dve.wait_ge(f_h, NT)
            tail(0, True, first=True)
            with dve.Fori(1, G // 2 - 1) as kk:
                tail(kk, True)
            tail(G // 2 - 1, False)


def dense_path(nc, ctx, c):
    N, H, O, NT, CH, NC = (c[k] for k in ("N", "H", "O", "NT", "CH", "NC"))
    w_sb, wst, ident, rstd, nmr, flag, x_t, out_t, adj_t = (
        c[k] for k in ("w_sb", "wst", "ident", "rstd", "nmr", "flag", "x_t", "out_t", "adj_t"))

    def sem(name):
        return ctx.enter_context(nc.semaphore(name))

    A = Arena(c["arena"])
    h = A.take([NT, P])
    big = A.take([H * NT * P])
    src_all = big.rearrange("p (h t i) -> p h t i", h=H, t=NT)
    proj = big.rearrange("p (t h o) -> p t h o", t=NT, h=H)
    nat = [A.take([CH * P]) for b in range(2)]
    z = A.take([H, CH, P])
    hc = A.take([P])
    hT = A.take([P])
    w_bc = A.take([H, P])
    src_row = A.take([H, P])
    st = A.take([NT, 2 * H])
    smax = A.take([H])
    nsmax = A.take([NC, H])
    csum = A.take([NC, H])
    nmax = A.take([NT, H])
    rsum = A.take([NT, H])
    xrow = A.take([O])
    fin = A.take([O])
    v = A.take([H, O])
    e = A.take([H, O])

    pT = [c["psum"][b][:, :].rearrange("p (c i) -> p c i", i=P) for b in range(2)]
    pW = c["psum"][2][:, 0:512].rearrange("p (h i) -> p h i", h=H)
    pH = c["psum"][2][:, 512:512 + P]
    pO = c["psum"][3][:, 0:512].rearrange("p (h i) -> p h i", h=H)

    d_h0 = sem("d_x_landed")
    d_h = sem("d_h_ready")
    d_wbc = sem("d_wbc")
    d_hc = sem("d_hc_copied")
    d_hps = sem("d_h_turned")
    d_hT = sem("d_hT_copied")
    d_small = sem("d_small_products")
    d_small_out = sem("d_small_products_read")
    d_nat = [sem(f"d_nat{b}_landed") for b in range(2)]
    d_turn = sem("d_adj_turned")
    d_zfree = sem("d_z_free")
    d_u = sem("d_u")
    d_l = sem("d_lrelu")
    d_z = sem("d_z_masked")
    d_s = sem("d_z_shifted")
    d_u2 = sem("d_step_max")
    d_e = sem("d_exp")
    d_comb = sem("d_combine")
    d_combe = sem("d_combine_exp")
    d_v = sem("d_final_sum")
    d_ve = sem("d_final_exp")
    d_f = sem("d_final_steps")
    d_fin = sem("d_final_ready")
    d_x = sem("d_xrow_landed")
    d_out = sem("d_out_stored")

    S1 = NT * NC
    COMB = 4
    FINAL = 4

    def dense(eng, program):
        go = eng.value_load(flag[0:1, 0:1], min_val=0, max_val=1)
        with eng.If(go > 0):
            program(eng)

    def dense_sync(sp):
        sp.dma_start(h, x_t).then_inc(d_h0, 16)
        sp.sem_inc(d_out, 16)
        with sp.Fori(0, NT) as j:
            with sp.Fori(0, NC // 2) as c:
                for b in range(2):
                    n = j * NC + c * 2 + b
                    sp.wait_ge(d_turn, n + 1)
                    sp.dma_start(nat[b].rearrange("p (c j) -> p c j", c=CH),
                                 adj_t[:, bass.ds((c * 2 + b) * CH, CH), bass.ds(j * P, P)]).then_inc(d_nat[b], 16)
        with sp.Fori(0, NT) as t:
            sp.wait_ge(d_fin, t + 1)
            sp.dma_start(xrow, x_t[:, t, :]).then_inc(d_x, 16)
            with sp.Fori(0, NC // 2) as g:
                for b in range(2):
                    n = t * NC + g * 2 + b + S1
                    sp.wait_ge(d_turn, n + 1)
                    sp.dma_start(nat[b], adj_t[:, t, bass.ds((g * 2 + b) * CH * P, CH * P)]).then_inc(d_nat[b], 16)
            sp.wait_ge(d_fin, t + 2)
            sp.dma_start(out_t[:, t, :], fin).then_inc(d_out, 16)
        sp.wait_ge(d_out, (NT + 1) * 16)

    def dense_tensor(pe):
        def turn_h(k):
            pe.wait_ge(d_hc, k + 1)
            pe.transpose(pH, hc, ident[:, :]).then_inc(d_hps, 1)
            pe.wait_ge(d_hT, k + 1)

        def spread_src():
            for hd in range(H):
                mm = pe.matmul(pW[:, hd, :], w_bc[:, hd, :], hT, start=True, stop=True, skip_group_check=True)
            return mm

        def turn_adj(n, b, cycle):
            pe.wait_ge(d_nat[b], (cycle + 1) * 16)
            pe.wait_ge(d_z, n + 1)
            for c in range(CH):
                mm = pe.transpose(pT[b][:, c, :], nat[b][:, c * P:(c + 1) * P], ident[:, :])
            mm.then_inc(d_turn, 1)

        pe.sem_inc(d_turn, 2)
        pe.wait_ge(d_wbc, 1)
        with pe.Fori(0, NT) as t:
            turn_h(t)
            spread_src()
            pe.matmul(pH[:, 0:2 * H], hT, wst[:, :], start=True, stop=True).then_inc(d_small, 1)
        with pe.Fori(0, NT) as j:
            with pe.Fori(0, NC // 2) as c:
                for b in range(2):
                    turn_adj(j * NC + c * 2 + b, b, j * (NC // 2) + c)
        with pe.Fori(0, NT) as t:
            turn_h(t + NT)
            pe.matmul(pW[:, :, :], hT, w_sb[:, :, :].rearrange("f h o -> f (h o)"),
                      start=True, stop=True).then_inc(d_small, 1)
        with pe.Fori(0, NT) as t:
            turn_h(t + 2 * NT)
            spread_src().then_inc(d_small, 1)
            pe.wait_ge(d_v, t + 1)
            for gg in range(NC // 2):
                for b in range(2):
                    g = gg * 2 + b
                    n = t * NC + g + S1
                    turn_adj(n, b, (t + NT) * (NC // 2) + gg)
                    pe.wait_ge(d_e, t * NC + g + 1)
                    for c in range(CH):
                        for hd in range(H):
                            mm = pe.matmul(pO[:, hd, :], z[:, hd, c, :], proj[:, g * CH + c, hd, :],
                                           start=(g == 0 and c == 0 and hd == 0), stop=(g == NC - 1 and c == CH - 1),
                                           skip_group_check=True)
                    mm.then_inc(d_zfree, 1)

    def dense_scalar(act):
        def copy_h(k, t):
            act.copy(hc, h[:, t, :]).then_inc(d_hc, 1)
            act.wait_ge(d_hps, k + 1)
            act.copy(hT, pH).then_inc(d_hT, 1)
            act.wait_ge(d_small, k + 1)
        act.wait_ge(d_h, NT + 1)
        with act.Fori(0, NT) as t:
            copy_h(t, t)
            act.copy(src_all[:, :, t, :], pW[:, :, :])
            act.copy(st[:, t, :], pH[:, 0:2 * H]).then_inc(d_small_out, 1)
        with act.Fori(0, NT) as j:
            with act.Fori(0, NC) as c:
                n = j * NC + c
                act.wait_ge(d_s, n + 1)
                for hd in range(H):
                    ins = act.activation(z[:, hd], z[:, hd], ACT.Exp, bias=nsmax[:, c, hd:hd + 1],
                                         accum_out=csum[:, c, hd:hd + 1])
                ins.then_inc(d_zfree, 1)
            act.wait_ge(d_comb, j * COMB + 2)
            act.activation(nsmax, nsmax, ACT.Exp).then_inc(d_combe, 1)
        with act.Fori(0, NT) as t:
            copy_h(t + NT, t)
            act.wait_ge(d_comb, NT * COMB + t + 2)
        with act.Fori(0, NT) as t:
            copy_h(t + 2 * NT, t)
            act.copy(src_row[:, :, :], pW[:, :, :]).then_inc(d_small_out, 1)
            with act.Fori(0, NC) as g:
                n = t * NC + g + S1
                act.wait_ge(d_s, n + 1)
                act.activation(z[:, :, :, :], z[:, :, :, :], ACT.Exp).then_inc(d_e, 1)
            act.wait_ge(d_v, t + 2)
            act.activation(e[:, :, :], v[:, :, :], ACT.Exp).then_inc(d_ve, 1)

    def dense_vector(dve):
        def scores(n, src, tgt, T):
            dve.wait_ge(d_zfree, n + 1)
            dve.tensor_tensor(z[:, :, :, :], src, tgt, ALU.add).then_inc(d_u, 1)
            dve.wait_ge(d_u, n + 1)
            dve.scalar_tensor_tensor(z[:, :, :, :], z[:, :, :, :], SLOPE, z[:, :, :, :],
                                     ALU.mult, ALU.max).then_inc(d_l, 1)
            dve.wait_ge(d_l, n + 1)
            dve.wait_ge(d_turn, n + 3)
            dve.tensor_tensor(z[:, :, :, :], z[:, :, :, :],
                              T[:, :, :].rearrange("p (g c) i -> p g c i", g=1).to_broadcast([P, H, CH, P]),
                              ALU.add).then_inc(d_z, 1)
            dve.wait_ge(d_z, n + 3)

        dve.wait_ge(d_h0, 16)
        with dve.Fori(0, NT) as t:
            dve.tensor_scalar(h[:, t, :], h[:, t, :], rstd[:, bass.ds(t, 1)], nmr[:, bass.ds(t, 1)],
                              ALU.mult, ALU.add).then_inc(d_h, 1)
        dve.wait_ge(d_h, NT)
        dve.tensor_scalar(h, h, 0.0, None, ALU.max).then_inc(d_h, 1)
        dve.sem_inc(d_z, 2)
        dve.sem_inc(d_zfree, 1)
        dve.sem_inc(d_v, 1)
        dve.sem_inc(d_fin, 1)
        for hd in range(H):
            ins = dve.tensor_copy(w_bc[:, hd, :], wst[:, hd:hd + 1].to_broadcast([P, P]))
        ins.then_inc(d_wbc, 1)
        dve.wait_ge(d_small_out, NT)
        with dve.Fori(0, NT) as j:
            with dve.Fori(0, NC // 2) as cc:
                for b in range(2):
                    c = cc * 2 + b
                    n = j * NC + c
                    scores(n, src_all[:, :, bass.ds(c * CH, CH), :],
                           st[:, j, H:2 * H].unsqueeze(2).unsqueeze(3).to_broadcast([P, H, CH, P]), pT[b])
                    dve.tensor_reduce(smax, z[:, :, :, :].rearrange("p h c i -> p h (c i)"), AX.X,
                                      ALU.max).then_inc(d_u2, 1)
                    dve.wait_ge(d_u2, n + 1)
                    dve.tensor_scalar(nsmax[:, c, :], smax, -1.0, None, ALU.mult).then_inc(d_s, 1)
            dve.wait_ge(d_zfree, j * NC + NC + 1)
            dve.tensor_reduce(nmax[:, j, :], nsmax.rearrange("p c h -> p h c"), AX.X,
                              ALU.min).then_inc(d_comb, 1)
            dve.wait_ge(d_comb, j * COMB + 1)
            dve.scalar_tensor_tensor(nsmax, nsmax, -1.0,
                                     nmax[:, j, :].unsqueeze(1).to_broadcast([P, NC, H]),
                                     ALU.mult, ALU.add).then_inc(d_comb, 1)
            dve.wait_ge(d_combe, j + 1)
            dve.tensor_tensor(csum[:, :, :], csum[:, :, :], nsmax, ALU.mult).then_inc(d_comb, 1)
            dve.wait_ge(d_comb, j * COMB + 3)
            dve.tensor_reduce(rsum[:, j, :], csum[:, :, :].rearrange("p c h -> p h c"), AX.X,
                              ALU.add).then_inc(d_comb, 1)
        dve.wait_ge(d_comb, NT * COMB)
        dve.reciprocal(rsum, rsum).then_inc(d_comb, 1)
        dve.wait_ge(d_comb, NT * COMB + 1)
        with dve.Fori(0, NT) as t:
            dve.wait_ge(d_small, t + NT + 1)
            dve.tensor_tensor(proj[:, t], pW[:, :, :], rsum[:, t, :].unsqueeze(2).to_broadcast([P, H, O]),
                              ALU.mult).then_inc(d_comb, 1)
        with dve.Fori(0, NT) as t:
            dve.wait_ge(d_small_out, t + NT + 1)
            for gg in range(NC // 2):
                for b in range(2):
                    n = t * NC + gg * 2 + b + S1
                    tiles = slice((gg * 2 + b) * CH, (gg * 2 + b + 1) * CH)
                    scores(n, src_row[:, :, :].unsqueeze(2).to_broadcast([P, H, CH, P]),
                           st[:, tiles, H:2 * H].rearrange("p c h -> p h c").unsqueeze(3).to_broadcast([P, H, CH, P]),
                           pT[b])
                    dve.tensor_tensor(z[:, :, :, :], z[:, :, :, :],
                                      nmax[:, tiles, :].rearrange("p c h -> p h c").unsqueeze(3).to_broadcast([P, H, CH, P]),
                                      ALU.add).then_inc(d_s, 1)
            dve.wait_ge(d_zfree, (t + 1) * NC + S1 + 1)
            dve.tensor_tensor(v[:, :, :], pO[:, :, :], h[:, t, :].unsqueeze(1).to_broadcast([P, H, O]),
                              ALU.add).then_inc(d_v, 1)
            dve.wait_ge(d_ve, t + 1)
            dve.tensor_scalar(e[:, :, :], e[:, :, :], 1.0, -1.0, ALU.min, ALU.add).then_inc(d_f, 1)
            dve.wait_ge(d_f, t * FINAL + 1)
            dve.tensor_tensor(v[:, :, :], v[:, :, :], e[:, :, :], ALU.max).then_inc(d_f, 1)
            dve.wait_ge(d_f, t * FINAL + 2)
            dve.tensor_tensor(v[:, 0:2, :], v[:, 0:2, :], v[:, 2:4, :], ALU.add).then_inc(d_f, 1)
            dve.wait_ge(d_f, t * FINAL + 3)
            dve.tensor_tensor(v[:, 0, :], v[:, 0, :], v[:, 1, :], ALU.add).then_inc(d_f, 1)
            dve.wait_ge(d_f, t * FINAL + 4)
            dve.wait_ge(d_x, (t + 1) * 16)
            dve.wait_ge(d_out, (t + 1) * 16)
            dve.scalar_tensor_tensor(fin, v[:, 0, :], 1.0 / H, xrow, ALU.mult, ALU.add).then_inc(d_fin, 1)

    with nc.Block() as block:
        @block.sync
        def _(sp):
            dense(sp, dense_sync)

        @block.tensor
        def _(pe):
            dense(pe, dense_tensor)

        @block.scalar
        def _(act):
            dense(act, dense_scalar)

        @block.vector
        def _(dve):
            dense(dve, dense_vector)


_INS = ["x", "adj", "L0_gnn_W", "L0_gnn_a_src", "L0_gnn_a_tgt"]


def kernel(**inputs):
    import numpy as np
    import concourse.bacc as bacc
    from concourse.bass_utils import run_bass_kernel_spmd

    nc = bacc.Bacc("TRN2", target_bir_lowering=False, num_devices=1)
    arrays, args = {}, []
    for name in _INS:
        a = np.ascontiguousarray(inputs[name])
        arrays[f"in_{name}"] = a
        args.append(nc.dram_tensor(f"in_{name}", a.shape, mybir.dt.from_np(a.dtype), kind="ExternalInput").ap())
    shape = inputs["x"].shape
    args.append(nc.dram_tensor("out", shape, F32, kind="ExternalOutput").ap())
    gat_kernel(nc, *args)
    r = run_bass_kernel_spmd(nc, [arrays], core_ids=[0])
    return r.results[0]["out"]
```
